# Optimizing a Trainium2 kernel written in Bass

```python
import numpy as np
import jax
import jax.numpy as jnp

def _softmax(x, axis=-1):
    return jax.nn.softmax(x, axis=axis)

def _gelu(x):
    return jax.nn.gelu(x, approximate=True)

def _silu(x):
    return jax.nn.silu(x)

def _sigmoid(x):
    return jax.nn.sigmoid(x)

def _layernorm(x, axis=-1, eps=1e-05):
    m = jnp.mean(x, axis=axis, keepdims=True)
    v = jnp.var(x, axis=axis, keepdims=True)
    return (x - m) / jnp.sqrt(v + eps)

def _scatter_add(tgt, idx, src, axis=0):
    return tgt.at[idx].add(src)

def _segment_sum(src, seg, n):
    return jax.ops.segment_sum(src, seg, n)
kernel_name = 'mk_gnn_ffn_d1_gnn_r8_61fc6c'

def setup_inputs(seed: int=0):
    np.random.seed(seed)
    _w = jnp.asarray

    def _rec_inputs():
        import jax
        import jax.numpy as jnp
        _gk = jax.random.key(seed)
        x = -0.0005963 + 1.001 * jax.random.normal(jax.random.fold_in(_gk, 1), (384, 1024), jnp.float32)
        src = jax.random.randint(jax.random.fold_in(_gk, 2), (12288,), 0, 384, jnp.int32)
        dst = jnp.minimum((384 * jax.random.uniform(jax.random.fold_in(_gk, 3), (12288,)) ** 2.0).astype(jnp.int32), 3071)
        _o = jnp.argsort(dst, stable=True)
        src = src[_o]
        dst = dst[_o]
        edge_type_5 = jax.random.randint(jax.random.fold_in(_gk, 12), (12288,), 0, 5, jnp.int32)
        return (x, src, dst, edge_type_5)
    x, src, dst, edge_type_5 = _rec_inputs()

    def _L0_gnn_setup():
        import jax, jax.numpy as jnp
        import numpy as np
        N = 384
        E = 12288
        IN_F = 1024
        OUT_F = 1024
        H = 16
        D = OUT_F // H
        NUM_ETYPES = 4

        def _build_mask(edge_index, edge_type, edge_type_weights, dtype):
            src, dst = (edge_index[0], edge_index[1])
            w = jax.nn.softplus(edge_type_weights)
            mask = jnp.full((N, N), -jnp.inf, dtype=dtype)
            mask = mask.at[src, dst].set(w[edge_type - 1])
            diag = jnp.diagonal(mask)
            idx = jnp.arange(N)
            mask = mask.at[idx, idx].set(jnp.where(jnp.isneginf(diag), w[3], diag))
            return mask
        key = jax.random.key(seed)
        ks = jax.random.split(key, 20)
        p = lambda k, shape: jax.random.normal(k, shape, dtype=jnp.float32) * 0.02
        return {'x': jax.random.normal(ks[0], (N, IN_F), dtype=jnp.float32), 'edge_index': jax.random.randint(ks[1], (2, E), 0, N), 'edge_type': jax.random.randint(ks[2], (E,), 1, NUM_ETYPES + 1), 'edge_type_weights': jnp.ones((NUM_ETYPES,), jnp.float32) + 0.1 * jax.random.normal(ks[3], (NUM_ETYPES,), dtype=jnp.float32), 'wq': p(ks[4], (OUT_F, IN_F)), 'bq': p(ks[5], (OUT_F,)), 'wk': p(ks[6], (OUT_F, IN_F)), 'bk': p(ks[7], (OUT_F,)), 'wv': p(ks[8], (OUT_F, IN_F)), 'bv': p(ks[9], (OUT_F,)), 'wiq': p(ks[10], (OUT_F, OUT_F)), 'biq': p(ks[11], (OUT_F,)), 'wik': p(ks[12], (OUT_F, OUT_F)), 'bik': p(ks[13], (OUT_F,)), 'wiv': p(ks[14], (OUT_F, OUT_F)), 'biv': p(ks[15], (OUT_F,)), 'wo': p(ks[16], (OUT_F, OUT_F)), 'bo': p(ks[17], (OUT_F,))}
    _L0_gnn_all = _L0_gnn_setup()
    _L0_gnn_in = {k: v for k, v in _L0_gnn_all.items() if k in ('edge_type_weights', 'wq', 'bq', 'wk', 'bk', 'wv', 'bv', 'wiq', 'biq', 'wik', 'bik', 'wiv', 'biv', 'wo', 'bo')}
    del _L0_gnn_all

    def _L0_ffn_setup():
        import jax, jax.numpy as jnp
        import numpy as np
        D_IN, D_HID = (1024, 512)

        def _ternary(key, shape):
            return jax.random.randint(key, shape, -1, 2).astype(jnp.float32)

        def _tlin(x, w, s):
            return jnp.einsum('bsi,oi->bso', x, w) * s
        key = jax.random.key(seed)
        ks = jax.random.split(key, 12)
        inv = lambda fan: 1.0 / np.sqrt(fan).astype(np.float32)
        return {'x': jax.random.normal(ks[0], (4, 256, D_IN), dtype=jnp.float32), 'w1_w': _ternary(ks[1], (D_HID, D_IN)), 'w1_s': jax.random.uniform(ks[2], (D_HID,), dtype=jnp.float32) * inv(D_IN), 'w2_w': _ternary(ks[3], (D_HID, D_IN)), 'w2_s': jax.random.uniform(ks[4], (D_HID,), dtype=jnp.float32) * inv(D_IN), 'h1_w': _ternary(ks[5], (D_HID, D_HID)), 'h1_s': jax.random.uniform(ks[6], (D_HID,), dtype=jnp.float32) * inv(D_HID), 'h2_w': _ternary(ks[7], (D_HID, D_HID)), 'h2_s': jax.random.uniform(ks[8], (D_HID,), dtype=jnp.float32) * inv(D_HID), 'w3_w': _ternary(ks[9], (D_IN, D_HID)), 'w3_s': jax.random.uniform(ks[10], (D_IN,), dtype=jnp.float32) * inv(D_HID)}
    _L0_ffn_all = _L0_ffn_setup()
    _L0_ffn_in = {k: v for k, v in _L0_ffn_all.items() if k in ('w1_w', 'w1_s', 'w2_w', 'w2_s', 'h1_w', 'h1_s', 'h2_w', 'h2_s', 'w3_w', 'w3_s')}
    del _L0_ffn_all
    return {'x': x, 'src': src, 'dst': dst, 'edge_type_5': edge_type_5, 'L0_gnn_edge_type_weights': _L0_gnn_in['edge_type_weights'], 'L0_gnn_wq': _L0_gnn_in['wq'], 'L0_gnn_bq': _L0_gnn_in['bq'], 'L0_gnn_wk': _L0_gnn_in['wk'], 'L0_gnn_bk': _L0_gnn_in['bk'], 'L0_gnn_wv': _L0_gnn_in['wv'], 'L0_gnn_bv': _L0_gnn_in['bv'], 'L0_gnn_wiq': _L0_gnn_in['wiq'], 'L0_gnn_biq': _L0_gnn_in['biq'], 'L0_gnn_wik': _L0_gnn_in['wik'], 'L0_gnn_bik': _L0_gnn_in['bik'], 'L0_gnn_wiv': _L0_gnn_in['wiv'], 'L0_gnn_biv': _L0_gnn_in['biv'], 'L0_gnn_wo': _L0_gnn_in['wo'], 'L0_gnn_bo': _L0_gnn_in['bo'], 'L0_ffn_w1_w': _L0_ffn_in['w1_w'], 'L0_ffn_w1_s': _L0_ffn_in['w1_s'], 'L0_ffn_w2_w': _L0_ffn_in['w2_w'], 'L0_ffn_w2_s': _L0_ffn_in['w2_s'], 'L0_ffn_h1_w': _L0_ffn_in['h1_w'], 'L0_ffn_h1_s': _L0_ffn_in['h1_s'], 'L0_ffn_h2_w': _L0_ffn_in['h2_w'], 'L0_ffn_h2_s': _L0_ffn_in['h2_s'], 'L0_ffn_w3_w': _L0_ffn_in['w3_w'], 'L0_ffn_w3_s': _L0_ffn_in['w3_s']}

def reference(x, src, dst, edge_type_5, L0_gnn_edge_type_weights, L0_gnn_wq, L0_gnn_bq, L0_gnn_wk, L0_gnn_bk, L0_gnn_wv, L0_gnn_bv, L0_gnn_wiq, L0_gnn_biq, L0_gnn_wik, L0_gnn_bik, L0_gnn_wiv, L0_gnn_biv, L0_gnn_wo, L0_gnn_bo, L0_ffn_w1_w, L0_ffn_w1_s, L0_ffn_w2_w, L0_ffn_w2_s, L0_ffn_h1_w, L0_ffn_h1_s, L0_ffn_h2_w, L0_ffn_h2_s, L0_ffn_w3_w, L0_ffn_w3_s):
    import jax
    import jax.numpy as jnp

    def _L0_gnn_ref(x, edge_index, edge_type, edge_type_weights, wq, bq, wk, bk, wv, bv, wiq, biq, wik, bik, wiv, biv, wo, bo):
        import jax, jax.numpy as jnp
        import numpy as np
        N = 384
        E = 12288
        IN_F = 1024
        OUT_F = 1024
        H = 16
        D = OUT_F // H
        NUM_ETYPES = 4

        def _build_mask(edge_index, edge_type, edge_type_weights, dtype):
            src, dst = (edge_index[0], edge_index[1])
            w = jax.nn.softplus(edge_type_weights)
            mask = jnp.full((N, N), -jnp.inf, dtype=dtype)
            mask = mask.at[src, dst].set(w[edge_type - 1])
            diag = jnp.diagonal(mask)
            idx = jnp.arange(N)
            mask = mask.at[idx, idx].set(jnp.where(jnp.isneginf(diag), w[3], diag))
            return mask
        q = x @ wq.T + bq
        k = x @ wk.T + bk
        v = x @ wv.T + bv
        q2 = (q @ wiq.T + biq).reshape(N, H, D).transpose(1, 0, 2)
        k2 = (k @ wik.T + bik).reshape(N, H, D).transpose(1, 0, 2)
        v2 = (v @ wiv.T + biv).reshape(N, H, D).transpose(1, 0, 2)
        mask = _build_mask(edge_index, edge_type, edge_type_weights, x.dtype)
        scale = 1.0 / np.sqrt(D).astype(np.float32)
        scores = jnp.einsum('hnd,hmd->hnm', q2, k2) * scale + mask[None]
        attn = jax.nn.softmax(scores, axis=-1)
        out = jnp.einsum('hnm,hmd->hnd', attn, v2)
        out = out.transpose(1, 0, 2).reshape(N, OUT_F)
        return out @ wo.T + bo

    def _L0_ffn_ref(x, w1_w, w1_s, w2_w, w2_s, h1_w, h1_s, h2_w, h2_s, w3_w, w3_s):
        import jax, jax.numpy as jnp
        import numpy as np
        D_IN, D_HID = (1024, 512)

        def _ternary(key, shape):
            return jax.random.randint(key, shape, -1, 2).astype(jnp.float32)

        def _tlin(x, w, s):
            return jnp.einsum('bsi,oi->bso', x, w) * s
        h = jax.nn.silu(_tlin(x, w1_w, w1_s)) * _tlin(x, w2_w, w2_s)
        h = jax.nn.gelu(_tlin(h, h1_w, h1_s), approximate=False)
        h = jax.nn.gelu(_tlin(h, h2_w, h2_s), approximate=False)
        return _tlin(h, w3_w, w3_s)
    edge_index = jnp.stack([src, dst])
    x = x + _L0_gnn_ref(_layernorm(x, axis=-1), edge_index, edge_type_5, L0_gnn_edge_type_weights, L0_gnn_wq, L0_gnn_bq, L0_gnn_wk, L0_gnn_bk, L0_gnn_wv, L0_gnn_bv, L0_gnn_wiq, L0_gnn_biq, L0_gnn_wik, L0_gnn_bik, L0_gnn_wiv, L0_gnn_biv, L0_gnn_wo, L0_gnn_bo)
    x = x + _L0_ffn_ref(_layernorm(x, axis=-1)[None], L0_ffn_w1_w, L0_ffn_w1_s, L0_ffn_w2_w, L0_ffn_w2_s, L0_ffn_h1_w, L0_ffn_h1_s, L0_ffn_h2_w, L0_ffn_h2_s, L0_ffn_w3_w, L0_ffn_w3_s)[0]
    return x

_drawn_inputs = setup_inputs


def setup_inputs(seed=0):
    import zlib

    import numpy as np

    out = dict(_drawn_inputs(seed))
    spreads = {}
    factors = {}
    for name, (base, spread) in spreads.items():
        noise = np.random.default_rng([zlib.crc32(name.encode()), seed]).standard_normal(out[name].shape)
        drawn = base * np.exp(spread * noise) if base else spread * noise
        out[name] = jnp.asarray(drawn.astype(out[name].dtype))
    for name, factor in factors.items():
        out[name] = (out[name] * factor).astype(out[name].dtype)
    return out
```

```python
from contextlib import ExitStack

import concourse.bass as bass
from concourse import mybir

F32 = mybir.dt.float32
F32R = mybir.dt.float32r
BF16 = mybir.dt.bfloat16
F16 = mybir.dt.float16
I32 = mybir.dt.int32
ALU = mybir.AluOpType
ACT = mybir.ActivationFunctionType

P = 128
NODES = 384
NT = NODES // P
FEAT = 1024
KT = FEAT // P
HALF = 512
HID = 512
HEADS = 16
HD = FEAT // HEADS
SCALE = 1.0 / 8.0
EDGES = 12288
ETILES = EDGES // P
CHUNKS = ETILES // 2
STEP_BITS = 5
EPS = 1e-5
ABSENT = 1e30
ROUNDER = 12582912.0
RING = 4
AHEAD = 3

U_V, U_IV, U_Q, U_K, U_AT, U_WO, U_F1, U_H1, U_H2, U_W3, UNITS = 0, 8, 16, 24, 32, 48, 56, 64, 66, 68, 72
C_BV, C_BQ, C_BK, C_BIQ, C_BIK, C_BIV = 0, 8, 16, 24, 40, 56
C_S1, C_S2, C_H1, C_H2, C_ALL = 72, 76, 80, 84, 88


def gnn_ffn(nc, x_in, src_dst, edge_cols, etw, weights, cols, bo, w3_s, codes_flat, out):
    src_nat, dst_nat = src_dst[0], src_dst[1]
    codes_nat = codes_flat.rearrange("(p f) -> p f", p=P)
    codes = codes_flat.rearrange("(g e) -> g e", g=8)
    with ExitStack() as ctx:
        def sem(name):
            return ctx.enter_context(nc.semaphore(name))

        at = [16512]

        def place(name, shape, dt, size):
            t = nc.alloc_sbuf_tensor_at(name, shape, dt, offset=at[0])
            n = size
            for d in shape[1:]:
                n *= d
            at[0] += (n + 31) // 32 * 32
            return t

        stage = place("stage", [P, RING, FEAT], F32, 4)
        w_hi = place("w_hi", [P, RING, FEAT], F32R, 4)
        w_lo = place("w_lo", [P, RING, FEAT], F32R, 4)
        xt_hi = place("xt_hi", [P, KT, NODES], F32R, 4)
        xt_lo = place("xt_lo", [P, KT, NODES], F32R, 4)
        qk_hi = place("qk_hi", [P, 2 * KT, NODES], F32R, 4)
        qk_lo = place("qk_lo", [P, 2 * KT, NODES], F32R, 4)
        v2 = place("v2", [P, NT, HEADS, 2 * HD], F32R, 4)
        xs = place("xs", [P, NT, FEAT], F32, 4)
        mask8 = place("mask8", [P, NT, NODES], F32, 4)
        rowvec = place("rowvec", [P, FEAT], F32, 4)
        ident = place("ident", [P, P], F32, 4)
        col = place("col", [P, C_ALL], F32, 4)
        stats = place("stats", [P, NT, 2, 6], F32, 4)
        mv = place("mv", [P, NT, 2], F32, 4)
        ve = place("ve", [P, NT], F32, 4)
        sd = place("sd", [P, NT], F32, 4)
        rstd = place("rstd", [P, NT], F32, 4)
        tmp3 = place("tmp3", [P, NT], F32, 4)
        negmax = place("negmax", [P, 2, NT], F32, 4)
        psums = place("psums", [P, 2, NT], F32, 4)
        rsums = place("rsums", [P, 2, NT], F32, 4)
        w8 = place("w8", [P, 4], F32, 4)
        spx = place("spx", [P, 4, 4], F32, 4)
        shared = at[0]

        xn = place("xn", [P, NT, FEAT], F32, 4)
        rows = place("rows", [P, 2, 6 * 256], F32, 4)
        oh_src = place("oh_src", [P, 4, NODES], BF16, 2)
        oh_dst = place("oh_dst", [P, 4, NODES], BF16, 2)
        later = place("later", [P, 256], BF16, 2)
        junk = place("junk", [P, 3, 256], BF16, 2)
        iota_i = place("iota_i", [P, NODES], I32, 4)
        iota_h = place("iota_h", [P, NODES], F16, 2)
        loops = place("loops", [P, 5 * P], BF16, 2)
        ident_b = place("ident_b", [P, P], BF16, 2)
        nat_i = place("nat_i", [P, 2, ETILES], I32, 4)
        nat_f = place("nat_f", [P, 2, ETILES], F32, 4)
        ncode = place("ncode", [P, ETILES], F32, 4)
        ecol_i = place("ecol_i", [P, 3, ETILES], I32, 4)
        ecol = place("ecol", [P, 3, ETILES], F32, 4)
        ecode = place("ecode", [P, ETILES], F32, 4)
        ebits = place("ebits", [P, ETILES], I32, 4)
        ebase_i = place("ebase_i", [P, ETILES], I32, 4)
        ebase = place("ebase", [P, ETILES], F32, 4)
        cnt = place("cnt", [P, 4], F32, 4)
        val = place("val", [P, 4], F32, 4)
        assert at[0] <= nc.sbuf_usable_end, at[0]
        at[0] = shared + NT * FEAT * 4
        dec = [place(f"dec{n}", [P, NT, NODES], F32 if n else I32, 4) for n in range(4)]
        at[0] = shared
        q2 = place("q2", [P, 2, 2, NODES], F32R, 4)
        k2_hi = place("k2_hi", [P, 2, 2, NODES], F32R, 4)
        k2_lo = place("k2_lo", [P, 2, 2, NODES], F32R, 4)
        pt_hi = place("pt_hi", [P, NT, NODES], F32R, 4)
        pt_lo = place("pt_lo", [P, NT, NODES], F32R, 4)
        prob = place("prob", [P, 2, NT, NODES], F32, 4)
        pv_t = place("pv_t", [P, NODES], F32, 4)
        pv_u = place("pv_u", [P, NODES], F32, 4)
        assert at[0] <= nc.sbuf_usable_end, at[0]
        at[0] = shared + NT * FEAT * 4
        ffn_g = place("ffn_g", [P, 2, NODES], F32, 4)
        ffn_h = place("ffn_h", [P, 2, NODES], F32, 4)
        yt = place("yt", [P, 2 * NT, HALF], F32, 4)

        bank = [ctx.enter_context(nc.psum_tensor(f"bank{b}", [P, HALF], F32)) for b in range(8)]

        x_sem = [sem(f"x_sem{s}") for s in range(NT)]
        cols_in = sem("cols_in")
        etw_in = sem("etw_in")
        nat_in = sem("nat_in")
        ecol_in = sem("ecol_in")
        bo_in = sem("bo_in")
        w3s_in = sem("w3s_in")
        codes_out = sem("codes_out")
        rows_in = [sem("rows_in0"), sem("rows_in1")]
        w_in = [sem(f"w_in{r}") for r in range(RING)]
        consts = sem("consts")
        hi_ready = sem("hi_ready")
        lo_ready = sem("lo_ready")
        unit_used = sem("unit_used")
        act_hi = sem("act_hi")
        act_lo = sem("act_lo")
        turned = sem("turned")
        ln_dve = sem("ln_dve")
        ln_sd = sem("ln_sd")
        normed = sem("normed")
        tok_done = sem("tok_done")
        v2_hi = sem("v2_hi")
        v2_lo = sem("v2_lo")
        resid = sem("resid")
        xbo = sem("xbo")
        code_nat = sem("code_nat")
        e_ready = sem("e_ready")
        sp_act = sem("sp_act")
        cmp_done = sem("cmp_done")
        val_ready = sem("val_ready")
        onehot = sem("onehot")
        edges_used = sem("edges_used")
        decoded = sem("decoded")
        k2_act = sem("k2_act")
        k2_ready = sem("k2_ready")
        q2_act = sem("q2_act")
        q2_ready = sem("q2_ready")
        s_done = sem("s_done")
        masked = sem("masked")
        exped = sem("exped")
        rsum = sem("rsum")
        prob_ready = sem("prob_ready")
        scores_seen = sem("scores_seen")
        sums_seen = sem("sums_seen")
        pt_done = sem("pt_done")
        pt_h = sem("pt_h")
        pt_l = sem("pt_l")
        pv_done = sem("pv_done")
        pv_half = sem("pv_half")
        pv_sum = sem("pv_sum")
        ot_h = sem("ot_h")
        ot_l = sem("ot_l")
        f_act = sem("f_act")
        f_mul = sem("f_mul")
        f_hi = sem("f_hi")
        f_lo = sem("f_lo")
        y_mul = sem("y_mul")
        y_ready = sem("y_ready")
        out_done = sem("out_done")
        st_done = sem("st_done")
        aggr_done = sem("aggr_done")
        src_ready = sem("src_ready")
        h_done = sem("h_done")
        ebase_b = ebase[:].bitcast(I32)

        def f32(ap):
            return ap.bitcast(F32)

        def rows_of(g):
            return codes[g].partition_broadcast(P)

        def ahead(g, uu):
            return RING * g + uu + AHEAD, (uu + AHEAD) % RING, g + 1 + (uu + AHEAD) // RING

        block = ctx.enter_context(nc.Block())

        @block.sync
        def _(sp):
            for s in range(NT):
                sp.dma_start(xs[:, s], x_in[s * P:(s + 1) * P, :]).then_inc(x_sem[s], 16)
            for u in range(RING):
                sp.dma_start(stage[:, u], weights[u]).then_inc(w_in[u], 16)

            def load_group(g, rows_slot):
                for uu in range(RING):
                    sp.wait_ge(lo_ready, RING * g + uu + 1)
                    sp.dma_start(stage[:, uu], weights[RING * g + RING + uu]).then_inc(w_in[uu], 16)
                    if uu == 1 and rows_slot is not None:
                        sp.wait_ge(cmp_done, 12 * g)
                        sp.dma_start(rows[:, rows_slot], rows_of(g + 1)).then_inc(rows_in[rows_slot], 16)

            load_group(0, None)
            with sp.Fori(0, 3) as i:
                load_group(2 * i + 1, 0)
                load_group(2 * i + 2, 1)
            with sp.Fori(7, UNITS // RING - 1) as g:
                load_group(g, None)
            sp.wait_ge(xbo, NT)
            sp.dma_start(rowvec[:], w3_s.partition_broadcast(P)).then_inc(w3s_in, 16)
            for n in range(2 * NT):
                h, s = n // NT, n % NT
                sp.wait_ge(y_ready, n + 1)
                sp.dma_start(out[s * P:(s + 1) * P, h * HALF:(h + 1) * HALF], yt[:, n]).then_inc(out_done, 16)
            sp.wait_ge(out_done, 16 * 2 * NT)

        @block.gpsimd
        def _(pool):
            pool.sem_inc(ot_l, 1)
            pool.memset(ident[:], 0.0).then_inc(consts, 1)
            pool.memset(ident_b[:], 0.0).then_inc(consts, 1)
            pool.memset(loops[:], 0.0).then_inc(consts, 1)
            pool.memset(later[:], 1.0).then_inc(consts, 1)
            pool.iota(iota_i[:], pattern=[[1, NODES]], base=0, channel_multiplier=0).then_inc(consts, 1)
            pool.iota(ebase_i[:], pattern=[[STEP_BITS, CHUNKS], [0, 2]], base=7,
                      channel_multiplier=0).then_inc(consts, 1)
            pool.wait_ge(consts, 6)
            pool.affine_select(out=ident[:], in_=ident[:], compare_op=ALU.not_equal, fill=1.0, base=0,
                               pattern=[[-1, P]], channel_multiplier=1).then_inc(consts, 1)
            pool.affine_select(out=ident_b[:], in_=ident_b[:], compare_op=ALU.not_equal, fill=1.0, base=0,
                               pattern=[[-1, P]], channel_multiplier=1).then_inc(consts, 1)
            pool.affine_select(out=loops[:, 2 * P:3 * P], in_=loops[:, 2 * P:3 * P], compare_op=ALU.not_equal,
                               fill=2.0 ** -122, base=0, pattern=[[-1, P]], channel_multiplier=1).then_inc(consts, 1)
            pool.affine_select(out=later[:], in_=later[:], compare_op=ALU.is_gt, fill=0.0, base=0,
                               pattern=[[1, 256]], channel_multiplier=-1).then_inc(consts, 1)
            pool.wait_ge(bo_in, 16)
            for s in range(NT):
                pool.wait_ge(normed, s + 1)
                pool.tensor_tensor(xs[:, s], xs[:, s], rowvec[:], ALU.add).then_inc(xbo, 1)

            def attention(i):
                for jj in range(2):
                    for hh in range(2):
                        h = 4 * i + 2 * jj + hh
                        pool.wait_ge(rsum, h + 1)
                        pool.sem_inc(sums_seen, 1)
                        for s in range(NT):
                            pool.tensor_scalar(prob[:, hh, s], prob[:, hh, s], rsums[:, hh, s:s + 1], None,
                                               ALU.mult).then_inc(prob_ready, 1)
                    pool.wait_ge(ot_h, 4 * i + 2 * jj + 2)
                    pool.tensor_tensor(xt_lo[:, 2 * i + jj], pv_u[:], f32(xt_hi[:, 2 * i + jj]),
                                       ALU.subtract).then_inc(ot_l, 1)

            with pool.Fori(0, 4) as i:
                attention(i)

        @block.scalar
        def _(act):
            act.dma_start(nat_i[:, 0], src_nat).then_inc(nat_in, 16)
            act.dma_start(nat_i[:, 1], dst_nat).then_inc(nat_in, 16)
            act.dma_start(ecol_i[:], edge_cols).then_inc(ecol_in, 16)
            act.dma_start(col[:], cols).then_inc(cols_in, 16)
            act.dma_start(spx[:, 0], etw.partition_broadcast(P)).then_inc(etw_in, 16)
            act.dma_start(rowvec[:], bo.partition_broadcast(P)).then_inc(bo_in, 16)
            act.wait_ge(code_nat, 1)
            act.dma_start(codes_nat, ncode[:]).then_inc(codes_out, 16)

            def split_hi(v, slot, count):
                act.wait_ge(w_in[slot], 16 * count)
                nc.scalar.activation(w_hi[:, slot], stage[:, slot], ACT.Copy).then_inc(hi_ready, 1)

            def split_ahead(g, uu):
                v, slot, count = ahead(g, uu)
                act.wait_ge(unit_used, v - (RING - 1) + 1)
                split_hi(v, slot, count)

            def layernorm(first):
                act.wait_ge(ln_dve, 1 if first else LN_STEPS + 1)
                nc.scalar.activation(sd[:], ve[:], ACT.Sqrt).then_inc(ln_sd, 1)

            def turned_hi(first):
                for f in range(KT):
                    act.wait_ge(turned, f + 1 + (0 if first else KT))
                    nc.scalar.activation(xt_hi[:, f], bank[2 + f % 2][:, 0:NODES], ACT.Copy).then_inc(act_hi, 1)

            layernorm(True)
            act.wait_ge(e_ready, 4)
            nc.scalar.activation(spx[:, 2], spx[:, 1], ACT.Exp).then_inc(sp_act, 1)
            act.wait_ge(sp_act, 1)
            nc.scalar.activation(spx[:, 3], spx[:, 2], ACT.Ln, bias=1.0).then_inc(sp_act, 1)
            act.wait_ge(codes_out, 16)
            for g in range(2):
                act.dma_start(rows[:, g], rows_of(g)).then_inc(rows_in[g], 16)
            for u in range(AHEAD):
                split_hi(u, u, 1)
            turned_hi(True)
            act.wait_ge(cols_in, 16)

            def project(g, uu, tile, bias):
                act.wait_ge(unit_used, RING * g + uu + 1 + 1)
                nc.scalar.activation(qk_hi[:, tile], bank[uu % 2][:, 0:NODES], ACT.Identity,
                                     bias=col[:, bass.ds(bias, 1)]).then_inc(act_hi, 1)

            with act.Fori(0, 2) as i:
                for uu in range(RING):
                    split_ahead(i, uu)
                    project(i, uu, RING * i + uu, C_BV + RING * i + uu)
            with act.Fori(0, 2) as i:
                for uu in range(RING):
                    split_ahead(i + 2, uu)
                for s in range(NT):
                    if s < NT - 1:
                        act.wait_ge(tok_done, 2 * i + s + 1)
                    else:
                        act.wait_ge(unit_used, U_IV + RING * i + RING + 1)
                    nc.scalar.activation(v2[:, s, bass.ds(8 * i, 8), 0:HD],
                                         bank[2 + s][:].rearrange("p (h d) -> p h d", d=HD),
                                         ACT.Copy).then_inc(v2_hi, 1)
            with act.Fori(0, 4) as i:
                for uu in range(RING):
                    split_ahead(i + 4, uu)
                    project(i + 4, uu, RING * i + uu, C_BQ + RING * i + uu)

            def keys_hi(j, jb):
                act.wait_ge(unit_used, U_AT + 2 * j + 1 + 1)
                for hh in range(2):
                    r = slice(64 * hh, 64 * hh + 64)
                    for half in range(2):
                        nc.scalar.activation(k2_hi[64 * half:64 * half + 64, jb, hh], bank[0][r, 0:NODES], ACT.Identity,
                                             bias=col[r, bass.ds(C_BIK + 2 * j + hh, 1)]).then_inc(k2_act, 1)

            def queries_hi(j, jb):
                act.wait_ge(unit_used, U_AT + 2 * j + 2 + 1)
                for hh in range(2):
                    r = slice(64 * hh, 64 * hh + 64)
                    nc.scalar.activation(q2[0:64, jb, hh], bank[1][r, 0:NODES], ACT.Identity,
                                         bias=col[r, bass.ds(C_BIQ + 2 * j + hh, 1)]).then_inc(q2_act, 1)

            def exps(h, hh):
                for s in range(NT):
                    act.wait_ge(masked, 3 * h + s + 1)
                    nc.scalar.activation(prob[:, hh, s], prob[:, hh, s], ACT.Exp, scale=-1.0,
                                         bias=negmax[:, hh, s:s + 1], accum_out=psums[:, hh, s:s + 1]).then_inc(exped, 1)

            def probs_t(h, hh):
                for m in range(NT):
                    act.wait_ge(pt_done, 3 * h + m + 1)
                    nc.scalar.activation(pt_hi[:, m], bank[5 + (3 * hh + m) % 2][:, 0:NODES], ACT.Copy).then_inc(pt_h, 1)

            def head_out(h, hh, tile):
                r = slice(64 * hh, 64 * hh + 64)
                act.wait_ge(pv_done, h + 1)
                act.wait_ge(pv_sum, h + 1)
                nc.scalar.activation(pv_t[0:64, :], bank[7][64:128, 0:NODES], ACT.Identity,
                                     bias=col[64:128, bass.ds(C_BIV + h, 1)]).then_inc(pv_half, 1)
                act.wait_ge(pv_sum, h + 1 + 1)
                nc.scalar.activation(xt_hi[r, tile], pv_u[r, :], ACT.Copy).then_inc(ot_h, 1)

            split_ahead(8, 0)
            keys_hi(0, 0)
            split_ahead(8, 1)
            queries_hi(0, 0)

            def attention(i, last):
                for jj in range(2):
                    a = 4 * i + 2 * jj
                    more = not (last and jj == 1)
                    exps(a, 0)
                    if more:
                        split_ahead(8 + i + jj, (2 + 2 * jj) % RING)
                        keys_hi(2 * i + jj + 1, (jj + 1) % 2)
                    exps(a + 1, 1)
                    probs_t(a, 0)
                    if more:
                        split_ahead(8 + i + jj, (3 + 2 * jj) % RING)
                    head_out(a, 0, 2 * i + jj)
                    probs_t(a + 1, 1)
                    if more:
                        queries_hi(2 * i + jj + 1, (jj + 1) % 2)
                    head_out(a + 1, 1, 2 * i + jj)

            with act.Fori(0, 3) as i:
                attention(i, False)
            attention(3, True)
            for g in (12, 13):
                for uu in range(RING):
                    split_ahead(g, uu)
            layernorm(False)
            turned_hi(False)

            def hidden_hi(n, tile):
                act.wait_ge(f_mul, n + 1) if n < 4 else act.wait_ge(f_act, n + 1)
                src = ffn_h if n < 4 else ffn_g
                nc.scalar.activation(qk_hi[:, tile], src[:, n % 2], ACT.Copy).then_inc(f_hi, 1)

            for j in range(4):
                split_ahead(14 + j // 2, 2 * (j % 2))
                act.wait_ge(unit_used, U_F1 + 2 * j + 1 + 1)
                if j >= 2:
                    act.wait_ge(f_mul, j - 1)
                nc.scalar.activation(ffn_g[:, j % 2], bank[2 * (j % 2)][:, 0:NODES], ACT.Silu,
                                     scale=col[:, C_S1 + j:C_S1 + j + 1]).then_inc(f_act, 1)
                split_ahead(14 + j // 2, 2 * (j % 2) + 1)
                hidden_hi(j, j)
            for n in range(4, 12):
                layer, o = (n - 4) // 4, n % 4
                if n % 2 == 0 and n // 2 - 2 + U_H1 + AHEAD < UNITS:
                    split_ahead(16, n // 2 - 2)
                act.wait_ge(h_done, n - 3)
                act.wait_ge(f_lo, n - 1)
                nc.scalar.activation(ffn_g[:, n % 2], bank[n % 4][:, 0:NODES], ACT.Gelu,
                                     scale=col[:, C_H1 + n - 4:C_H1 + n - 3]).then_inc(f_act, 1)
                hidden_hi(n, n)
            split_ahead(17, 0)

        @block.vector
        def _(dve):
            for counted in (v2_lo, pv_sum, resid):
                dve.sem_inc(counted, 1)

            def split_lo(v, slot):
                dve.wait_ge(hi_ready, v + 1)
                nc.vector.tensor_tensor(w_lo[:, slot], stage[:, slot], f32(w_hi[:, slot]),
                                        ALU.subtract).then_inc(lo_ready, 1)

            def split_ahead(g, uu):
                v, slot, _ = ahead(g, uu)
                split_lo(v, slot)

            links = [0]

            def link(ins, signal):
                links[0] += 1
                ins.then_inc(signal, 1)
                dve.wait_ge(signal, links[0])

            def stats_of(s, hf):
                return nc.vector.bn_stats(stats[:, s, hf], xs[:, s, hf * HALF:(hf + 1) * HALF])

            def layernorm(first, done):
                links[0] = 0 if first else LN_STEPS
                for s in range(NT):
                    last = nc.vector.bn_aggr(mv[:, s], stats[:, s].rearrange("p a b -> p (a b)"))
                last.then_inc(done, 1)
                dve.wait_ge(done, 1 if first else 2)
                link(nc.vector.tensor_scalar(ve[:], mv[:, :, 1], EPS, None, ALU.add), ln_dve)
                dve.wait_ge(ln_sd, 1 if first else 2)
                link(nc.vector.reciprocal(rstd[:], sd[:]), ln_dve)
                link(nc.vector.tensor_tensor(tmp3[:], rstd[:], rstd[:], ALU.mult), ln_dve)
                link(nc.vector.tensor_tensor(tmp3[:], tmp3[:], ve[:], ALU.mult), ln_dve)
                link(nc.vector.tensor_scalar(tmp3[:], tmp3[:], -0.5, 1.5, ALU.mult, ALU.add), ln_dve)
                link(nc.vector.tensor_tensor(rstd[:], rstd[:], tmp3[:], ALU.mult), ln_dve)
                for s in range(NT):
                    nc.vector.tensor_scalar(xn[:, s], xs[:, s], mv[:, s, 0:1], rstd[:, s:s + 1],
                                            ALU.subtract, ALU.mult).then_inc(normed, 1)

            def turned_lo(first):
                for f in range(KT):
                    dve.wait_ge(act_hi, f + 1 + (0 if first else 32))
                    nc.vector.tensor_tensor(xt_lo[:, f], bank[2 + f % 2][:, 0:NODES], f32(xt_hi[:, f]),
                                            ALU.subtract).then_inc(act_lo, 1)

            dve.wait_ge(nat_in, 32)
            nc.vector.tensor_copy(nat_f[:], nat_i[:]).then_inc(e_ready, 1)
            dve.wait_ge(e_ready, 1)
            nc.vector.scalar_tensor_tensor(out=ncode[:], in0=nat_f[:, 0], scalar=float(NODES), in1=nat_f[:, 1],
                                           op0=ALU.mult, op1=ALU.add).then_inc(code_nat, 1)
            for s in range(NT):
                dve.wait_ge(x_sem[s], 16)
                for hf in range(2):
                    last = stats_of(s, hf)
            last.then_inc(st_done, 1)
            dve.wait_ge(st_done, 1)
            layernorm(True, aggr_done)
            dve.wait_ge(ecol_in, 16)
            nc.vector.tensor_copy(ecol[:], ecol_i[:]).then_inc(e_ready, 1)
            dve.wait_ge(etw_in, 16)
            nc.vector.tensor_scalar(spx[:, 1], spx[:, 0], -1.0, None, ALU.mult).then_inc(e_ready, 1)
            dve.wait_ge(e_ready, 3)
            nc.vector.tensor_tensor(spx[:, 1], spx[:, 1], spx[:, 0], ALU.min).then_inc(e_ready, 1)
            nc.vector.scalar_tensor_tensor(out=ecode[:], in0=ecol[:, 0], scalar=float(NODES), in1=ecol[:, 1],
                                           op0=ALU.mult, op1=ALU.add).then_inc(e_ready, 1)
            nc.vector.tensor_scalar(ebase[:], ecol[:, 2], 0.0, 4.0, ALU.is_equal, ALU.mult).then_inc(e_ready, 1)
            dve.wait_ge(e_ready, 6)
            nc.vector.scalar_tensor_tensor(out=ebase[:], in0=ecol[:, 2], scalar=-1.0, in1=ebase[:],
                                           op0=ALU.add, op1=ALU.add).then_inc(e_ready, 1)
            dve.wait_ge(e_ready, 7)
            dve.wait_ge(consts, 10)
            nc.vector.tensor_tensor(ebits[:], ebase[:], ebase_i[:], ALU.add).then_inc(e_ready, 1)
            nc.vector.tensor_copy(iota_h[:], iota_i[:]).then_inc(e_ready, 1)
            dve.wait_ge(e_ready, 9)
            nc.vector.tensor_scalar(ebase_b, ebits[:], 23, None, ALU.logical_shift_left).then_inc(e_ready, 1)
            dve.wait_ge(e_ready, 10)
            for u in range(AHEAD):
                split_lo(u, u)
            turned_lo(True)
            dve.wait_ge(cols_in, 16)

            def edge_step(g, uu, slot):
                t0 = 12 * g + 3 * uu
                for d in range(3):
                    tl = 3 * uu + d
                    lo = 256 * (tl // 2) + P * (tl % 2)
                    w = 256 - P * (tl % 2)
                    nc.vector.scalar_tensor_tensor(
                        out=junk[:, d, 0:w], in0=rows[:, slot, lo:lo + w], scalar=ecode[:, bass.ds(t0 + d, 1)],
                        in1=later[:, 0:w], op0=ALU.is_equal, op1=ALU.mult, accum_out=cnt[:, d:d + 1]).then_inc(cmp_done, 1)
                for d in range(3):
                    dve.wait_ge(edges_used, t0 + d + 1)
                    nc.vector.tensor_scalar(oh_src[:, (3 * uu + d) % 4], iota_h[:], ecol[:, 0, bass.ds(t0 + d, 1)], None,
                                            ALU.is_equal).then_inc(src_ready, 1)
                    if d == 0:
                        dve.wait_ge(cmp_done, t0 + 3)
                        nc.vector.scalar_tensor_tensor(
                            out=val[:, 0:3], in0=cnt[:, 0:3], scalar=0.0, in1=ebase[:, bass.ds(t0, 3)],
                            op0=ALU.is_equal, op1=ALU.mult).then_inc(val_ready, 1)
                for d in range(3):
                    if d == 0:
                        dve.wait_ge(val_ready, 4 * g + uu + 1)
                    nc.vector.tensor_scalar(oh_dst[:, (3 * uu + d) % 4], iota_h[:], ecol[:, 1, bass.ds(t0 + d, 1)],
                                            val[:, d:d + 1], ALU.is_equal, ALU.mult).then_inc(onehot, 1)

            def rows_wait(slot, count):
                dve.wait_ge(rows_in[slot], 16 * count)

            def project_lo(n, uu, tile, bias):
                dve.wait_ge(act_hi, KT + n + 1)
                nc.vector.scalar_tensor_tensor(
                    out=qk_lo[:, tile], in0=bank[uu % 2][:, 0:NODES], scalar=col[:, bass.ds(bias, 1)],
                    in1=f32(qk_hi[:, tile]), op0=ALU.add, op1=ALU.subtract).then_inc(act_lo, 1)

            for g in range(2):
                rows_wait(g, 1)
                for uu in range(RING):
                    split_ahead(g, uu)
                    edge_step(g, uu, g)
                    project_lo(RING * g + uu, uu, RING * g + uu, C_BV + RING * g + uu)
            for g in range(2, 4):
                rows_wait(g % 2, 2)
                for uu in range(RING):
                    split_ahead(g, uu)
                    edge_step(g, uu, g % 2)
                for s in range(NT):
                    n = NT * (g - 2) + s
                    dve.wait_ge(v2_hi, n + 1)
                    heads = slice(8 * (g - 2), 8 * (g - 2) + 8)
                    nc.vector.tensor_tensor(v2[:, s, heads, HD:2 * HD], bank[2 + s][:].rearrange("p (h d) -> p h d", d=HD),
                                            f32(v2[:, s, heads, 0:HD]), ALU.subtract).then_inc(v2_lo, 1)
            with dve.Fori(0, 2) as i:
                for slot in range(2):
                    g = 2 * i + 4 + slot
                    rows_wait(slot, i + 3)
                    for uu in range(RING):
                        n = 8 * i + RING * slot + uu
                        split_ahead(g, uu)
                        edge_step(g, uu, slot)
                        project_lo(KT + n, uu, n, C_BQ + n)

            split_ahead(8, 0)
            links[0] = 0
            dve.wait_ge(edges_used, ETILES + 3 + 1)
            link(nc.vector.tensor_scalar(w8[:], spx[:, 0], 0.0, None, ALU.max), decoded)
            dve.wait_ge(sp_act, 2)
            link(nc.vector.tensor_tensor(w8[:], w8[:], spx[:, 3], ALU.add), decoded)
            link(nc.vector.tensor_scalar(w8[:], w8[:], 8.0, None, ALU.mult), decoded)
            d_i, d_e, d_q, d_m = dec
            for s in range(NT):
                nc.vector.tensor_copy(d_m[:, s], bank[5 + s][:, 0:NODES]).then_inc(decoded, 1)
                links[0] += 1
            dve.wait_ge(decoded, links[0])
            link(nc.vector.tensor_scalar(d_i[:], d_m[:].bitcast(I32), 23, None, ALU.logical_shift_right), decoded)
            link(nc.vector.tensor_scalar(mask8[:], d_m[:], 0.0, 1.0, ALU.is_gt, ALU.subtract), decoded)
            link(nc.vector.tensor_copy(d_e[:], d_i[:]), decoded)
            link(nc.vector.tensor_scalar(d_q[:], d_e[:], 0.2, -0.8, ALU.mult, ALU.add), decoded)
            link(nc.vector.tensor_scalar(d_q[:], d_q[:], ROUNDER, ROUNDER, ALU.add, ALU.subtract), decoded)
            link(nc.vector.scalar_tensor_tensor(out=d_e[:], in0=d_q[:], scalar=-5.0, in1=d_e[:],
                                                op0=ALU.mult, op1=ALU.add), decoded)
            for n in range(4):
                link(nc.vector.tensor_scalar(d_q[:], d_e[:], float(n + 2), w8[:, n:n + 1], ALU.is_equal, ALU.mult), decoded)
                out_ = mask8 if n == 3 else d_m
                if n == 0:
                    link(nc.vector.tensor_copy(d_m[:], d_q[:]), decoded)
                elif n < 3:
                    link(nc.vector.tensor_tensor(d_m[:], d_m[:], d_q[:], ALU.add), decoded)
                else:
                    link(nc.vector.tensor_tensor(d_m[:], d_m[:], d_q[:], ALU.add), decoded)
                    link(nc.vector.scalar_tensor_tensor(out=mask8[:], in0=mask8[:], scalar=ABSENT, in1=d_m[:],
                                                        op0=ALU.mult, op1=ALU.add), decoded)

            decode_steps = links[0]

            def keys_lo(j, jb):
                dve.wait_ge(k2_act, 4 * j + 4)
                for hh in range(2):
                    r = slice(64 * hh, 64 * hh + 64)
                    for half in range(2):
                        last = nc.vector.scalar_tensor_tensor(
                            out=k2_lo[64 * half:64 * half + 64, jb, hh], in0=bank[0][r, 0:NODES],
                            scalar=col[0:64, bass.ds(C_BIK + 2 * j + hh, 1)], in1=f32(k2_hi[0:64, jb, hh]),
                            op0=ALU.add, op1=ALU.subtract)
                last.then_inc(k2_ready, 1)

            def queries_lo(j, jb):
                dve.wait_ge(q2_act, 2 * j + 2)
                for hh in range(2):
                    r = slice(64 * hh, 64 * hh + 64)
                    last = nc.vector.scalar_tensor_tensor(
                        out=q2[64:128, jb, hh], in0=bank[1][r, 0:NODES],
                        scalar=col[0:64, bass.ds(C_BIQ + 2 * j + hh, 1)], in1=f32(q2[0:64, jb, hh]),
                        op0=ALU.add, op1=ALU.subtract)
                last.then_inc(q2_ready, 1)

            def mask_scores(h, hh):
                for s in range(NT):
                    dve.wait_ge(s_done, 3 * h + s + 1)
                    dve.sem_inc(scores_seen, 1)
                    nc.vector.tensor_tensor_reduce(prob[:, hh, s], bank[2 + s][:, 0:NODES], mask8[:, s], -SCALE, 3e38,
                                                   ALU.add, ALU.min, negmax[:, hh, s:s + 1]).then_inc(masked, 1)

            def recip(h, hh):
                dve.wait_ge(exped, 3 * h + 3)
                nc.vector.reciprocal(rsums[:, hh], psums[:, hh]).then_inc(rsum, 1)

            def probs_lo(h, hh):
                for m in range(NT):
                    dve.wait_ge(pt_h, 3 * h + m + 1)
                    nc.vector.tensor_tensor(pt_lo[:, m], bank[5 + (3 * hh + m) % 2][:, 0:NODES], f32(pt_hi[:, m]),
                                            ALU.subtract).then_inc(pt_l, 1)

            def head_sum(h, hh, j):
                r = slice(64 * hh, 64 * hh + 64)
                dve.wait_ge(pv_half, h + 1)
                dve.wait_ge(ot_l, j + 1)
                nc.vector.tensor_tensor(pv_u[r, :], bank[7][0:64, 0:NODES], pv_t[0:64, :], ALU.add).then_inc(pv_sum, 1)

            keys_lo(0, 0)
            split_ahead(8, 1)
            queries_lo(0, 0)

            def attention(i, last):
                for jj in range(2):
                    a = 4 * i + 2 * jj
                    more = not (last and jj == 1)
                    mask_scores(a, 0)
                    recip(a, 0)
                    if more:
                        split_ahead(8 + i + jj, (2 + 2 * jj) % RING)
                        keys_lo(2 * i + jj + 1, (jj + 1) % 2)
                    mask_scores(a + 1, 1)
                    probs_lo(a, 0)
                    recip(a + 1, 1)
                    if more:
                        split_ahead(8 + i + jj, (3 + 2 * jj) % RING)
                    head_sum(a, 0, 2 * i + jj)
                    probs_lo(a + 1, 1)
                    if more:
                        queries_lo(2 * i + jj + 1, (jj + 1) % 2)
                    head_sum(a + 1, 1, 2 * i + jj)

            with dve.Fori(0, 3) as i:
                attention(i, False)
            attention(3, True)
            for h in range(2):
                for uu in range(RING):
                    split_ahead(12 + h, uu)
                dve.wait_ge(xbo, NT)
                for s in range(NT):
                    if s < NT - 1:
                        dve.wait_ge(tok_done, 4 + 2 * h + s + 1)
                    else:
                        dve.wait_ge(unit_used, U_WO + RING * h + RING + 1)
                    xh = xs[:, s, h * HALF:(h + 1) * HALF]
                    nc.vector.tensor_tensor(xh, bank[2 + s][:], xh, ALU.add).then_inc(resid, 1)
                dve.wait_ge(resid, NT * h + NT + 1)
                for s in range(NT):
                    last = stats_of(s, h)
            last.then_inc(st_done, 1)
            dve.wait_ge(st_done, 2)
            layernorm(False, aggr_done)
            turned_lo(False)

            def hidden_lo(n):
                src = ffn_h if n < 4 else ffn_g
                dve.wait_ge(f_hi, n + 1)
                nc.vector.tensor_tensor(qk_lo[:, n], src[:, n % 2], f32(qk_hi[:, n]), ALU.subtract).then_inc(f_lo, 1)

            for j in range(4):
                split_ahead(14 + j // 2, 2 * (j % 2))
                split_ahead(14 + j // 2, 2 * (j % 2) + 1)
                dve.wait_ge(f_act, j + 1)
                dve.wait_ge(unit_used, U_F1 + 2 * j + 2 + 1)
                nc.vector.scalar_tensor_tensor(out=ffn_h[:, j % 2], in0=bank[2 * (j % 2) + 1][:, 0:NODES],
                                               scalar=col[:, C_S2 + j:C_S2 + j + 1], in1=ffn_g[:, j % 2],
                                               op0=ALU.mult, op1=ALU.mult).then_inc(f_mul, 1)
                hidden_lo(j)
            for n in range(4, 12):
                if n % 2 == 0 and n // 2 - 2 + U_H1 + AHEAD < UNITS:
                    split_ahead(16, n // 2 - 2)
                hidden_lo(n)
            split_ahead(17, 0)
            dve.wait_ge(w3s_in, 16)
            for n in range(2 * NT):
                h, s = n // NT, n % NT
                if s < NT - 1:
                    dve.wait_ge(tok_done, 8 + 2 * h + s + 1)
                else:
                    dve.wait_ge(unit_used, U_W3 + 2 * h + 2 + 1)
                nc.vector.tensor_tensor(yt[:, n], bank[2 + 3 * h + s][:], rowvec[:, h * HALF:(h + 1) * HALF],
                                        ALU.mult).then_inc(y_mul, 1)
                dve.wait_ge(y_mul, n + 1)
                nc.vector.tensor_tensor(yt[:, n], yt[:, n], xs[:, s, h * HALF:(h + 1) * HALF], ALU.add).then_inc(y_ready, 1)

        @block.tensor
        def _(pe):
            pe.sem_inc(unit_used, 1)
            pe.sem_inc(edges_used, 1)

            def turn(first):
                for f in range(KT):
                    if first and f >= 2:
                        pe.wait_ge(act_lo, f - 1)
                    if not first:
                        pe.wait_ge(act_lo, 32 + f - 1)
                    for s in range(NT):
                        if f == 0:
                            pe.wait_ge(normed, s + 1 + (0 if first else NT))
                        last = nc.tensor.transpose(bank[2 + f % 2][:, s * P:(s + 1) * P], xn[:, s, f * P:(f + 1) * P], ident[:])
                    last.then_inc(turned, 1)

            def by_weight(slot, offset, kt, acts, a0, dst, passes, tail=None):
                n, last_n = 0, 3 * kt - 1
                for k in range(kt):
                    w = slice(offset + k * P, offset + (k + 1) * P)
                    for wp, ap in ((w_hi, acts[0]), (w_hi, acts[1]), (w_lo, acts[0])):
                        if passes[0] <= n < passes[1]:
                            last = nc.tensor.matmul(dst[:, 0:NODES], wp[:, slot, w], ap[:, a0 + k], start=n == 0, stop=n == last_n)
                        n += 1
                return last

            ALLP = (0, 24)
            XT, QK = (xt_hi, xt_lo), (qk_hi, qk_lo)

            def by_nodes(slot, pair, pairs, acts, a0, banks, done, wait_bank):
                for s in range(NT):
                    wait_bank(s)
                    for k2 in range(2):
                        k = 2 * pair + k2
                        a = slice(s * P, (s + 1) * P)
                        c = slice(k2 * HALF, (k2 + 1) * HALF)
                        for m, (ap, wp) in enumerate(((acts[0], w_hi), (acts[0], w_lo), (acts[1], w_hi))):
                            last = nc.tensor.matmul(banks[s][:], ap[:, a0 + k, a], wp[:, slot, c],
                                                    start=k == 0 and m == 0, stop=k == 2 * pairs - 1 and m == 2)
                    if pair == pairs - 1 and s < NT - 1:
                        last.then_inc(done, 1)
                last.then_inc(unit_used, 1)

            def edges(g, uu):
                for d in range(3):
                    pe.wait_ge(onehot, 12 * g + 3 * uu + d + 1)
                    e = (3 * uu + d) % 4
                    for s in range(NT):
                        last = nc.tensor.matmul(bank[5 + s][:, 0:NODES], oh_src[:, e, s * P:(s + 1) * P], oh_dst[:, e],
                                                start=False, stop=True, skip_group_check=True)
                    last.then_inc(edges_used, 1)

            pe.wait_ge(consts, 10)
            turn(True)
            for s in range(NT):
                nc.tensor.matmul(bank[5 + s][:, 0:NODES], ident_b[:], loops[:, 2 * P - s * P:2 * P - s * P + NODES],
                                 start=True, stop=True, skip_group_check=True).then_inc(edges_used, 1)

            def project(g, uu, n, a0_acts):
                pe.wait_ge(lo_ready, RING * g + uu + 1)
                pe.wait_ge(act_lo, KT + n - 1)
                by_weight(uu, 0, KT, XT, 0, bank[uu % 2], ALLP).then_inc(unit_used, 1)
                edges(g, uu)

            pe.wait_ge(act_lo, KT)
            with pe.Fori(0, 2) as i:
                for uu in range(RING):
                    project(i, uu, RING * i + uu, None)
            pe.wait_ge(act_lo, 2 * KT)
            with pe.Fori(0, 2) as i:
                for uu in range(RING):
                    pe.wait_ge(lo_ready, U_IV + RING * i + uu + 1)
                    by_nodes(uu, uu, RING, QK, 0, bank[2:5], tok_done,
                             lambda s: pe.wait_ge(v2_lo, NT * i + 1) if uu == 0 and s == 0 else None)
                    edges(i + 2, uu)
            with pe.Fori(0, 4) as i:
                for uu in range(RING):
                    project(i + 4, uu, KT + RING * i + uu, None)

            pe.wait_ge(act_lo, 4 * KT)

            def inner(u, b, parts, ready, j):
                if parts[0] == 0:
                    pe.wait_ge(lo_ready, u + 1)
                    pe.wait_ge(ready, j)
                last = by_weight(u % RING, 0, KT, QK, KT * (1 - b), bank[b], parts)
                if parts[1] == 24:
                    last.then_inc(unit_used, 1)

            def scores(h):
                j = h // 2
                pe.wait_ge(k2_ready, j + 1)
                pe.wait_ge(q2_ready, j + 1)
                pe.wait_ge(masked, 3 * h)
                for s in range(NT):
                    for n, k2 in enumerate((k2_hi, k2_lo)):
                        last = nc.tensor.matmul(bank[2 + s][:, 0:NODES], q2[:, j % 2, h % 2, s * P:(s + 1) * P], k2[:, j % 2, h % 2],
                                                start=n == 0, stop=n == 1)
                    last.then_inc(s_done, 1)

            def turn_probs(h):
                pe.wait_ge(prob_ready, 3 * h + 3)
                for m in range(NT):
                    pe.wait_ge(pt_l, 3 * h if m < 2 else 3 * h + 1)
                    for s in range(NT):
                        last = nc.tensor.transpose(bank[5 + (3 * (h % 2) + m) % 2][:, s * P:(s + 1) * P],
                                                   prob[:, h % 2, s, m * P:(m + 1) * P], ident[:])
                    last.then_inc(pt_done, 1)

            def weigh(h):
                pe.wait_ge(pv_sum, h + 1)
                for m in range(NT):
                    pe.wait_ge(pt_l, 3 * h + m + 1)
                    for n, pt in enumerate((pt_hi, pt_lo)):
                        last = nc.tensor.matmul(bank[7][:, 0:NODES], v2[:, m, h], pt[:, m],
                                                start=m == 0 and n == 0, stop=m == NT - 1 and n == 1)
                last.then_inc(pv_done, 1)

            inner(U_AT, 0, (0, 24), k2_ready, 0)
            inner(U_AT + 1, 1, (0, 24), q2_ready, 0)
            for j in range(HEADS // 2):
                a, u = 2 * j, U_AT + 2 * j + 2
                more = j + 1 < HEADS // 2
                scores(a)
                if more:
                    inner(u, 0, (0, 24), k2_ready, j + 1)
                scores(a + 1)
                turn_probs(a)
                if more:
                    inner(u + 1, 1, (0, 12), q2_ready, j + 1)
                weigh(a)
                turn_probs(a + 1)
                if more:
                    inner(u + 1, 1, (12, 24), q2_ready, j + 1)
                weigh(a + 1)

            with pe.Fori(0, 2) as i:
                for uu in range(RING):
                    pe.wait_ge(lo_ready, U_WO + RING * i + uu + 1)
                    pe.wait_ge(ot_l, 2 * uu + 2 + 1)
                    by_nodes(uu, uu, RING, XT, 0, bank[2:5], tok_done,
                             lambda s: pe.wait_ge(resid, NT * i + 1) if uu == 0 and s == 0 else None)
            turn(False)
            pe.wait_ge(act_lo, 5 * KT)
            for j in range(4):
                for n in range(2):
                    u = U_F1 + 2 * j + n
                    pe.wait_ge(lo_ready, u + 1)
                    if j >= 2:
                        pe.wait_ge(f_mul, j - 1)
                    by_weight(u % RING, 0, KT, XT, 0, bank[2 * (j % 2) + n], ALLP).then_inc(unit_used, 1)
            for n in range(4, 12):
                u = U_H1 + (n - 4) // 2
                pe.wait_ge(lo_ready, u + 1)
                pe.wait_ge(f_lo, 4 if n < 8 else 8)
                last = by_weight(u % RING, HALF * (n % 2), 4, QK, 0 if n < 8 else 4, bank[n % 4], ALLP)
                last.then_inc(h_done, 1)
                if n % 2 == 1:
                    pe.wait_ge(h_done, n - 3)
                    pe.nop().then_inc(unit_used, 1)
            for h in range(2):
                for pair in range(2):
                    u = U_W3 + 2 * h + pair
                    pe.wait_ge(lo_ready, u + 1)
                    pe.wait_ge(f_lo, 12)
                    by_nodes(u % RING, pair, 2, QK, 8, bank[2 + 3 * h:5 + 3 * h], tok_done, lambda s: None)


LN_STEPS = 6


def host_units(w):
    import numpy as np

    def by_weight(a):
        o, i = a.shape
        per = FEAT // i
        return a.reshape(o // P // per, per, P, i // P, P).transpose(0, 4, 1, 3, 2).reshape(-1, P, FEAT)

    def by_nodes(a):
        o, i = a.shape
        return a.reshape(o // HALF, HALF, i // (2 * P), 2, P).transpose(0, 2, 4, 3, 1).reshape(-1, P, FEAT)

    def in_turn(a, b):
        return np.stack([by_weight(a), by_weight(b)], axis=1).reshape(-1, P, FEAT)

    units = [by_weight(w["L0_gnn_wv"]), by_nodes(w["L0_gnn_wiv"]), by_weight(w["L0_gnn_wq"]), by_weight(w["L0_gnn_wk"]),
             in_turn(w["L0_gnn_wik"], w["L0_gnn_wiq"]), by_nodes(w["L0_gnn_wo"]), in_turn(w["L0_ffn_w1_w"], w["L0_ffn_w2_w"]),
             by_weight(w["L0_ffn_h1_w"]), by_weight(w["L0_ffn_h2_w"]), by_nodes(w["L0_ffn_w3_w"])]
    return np.ascontiguousarray(np.concatenate(units))


def host_cols(w):
    import numpy as np

    def tiles(a):
        return a.reshape(-1, P).T

    def heads(a):
        return np.concatenate([a.reshape(HEADS, HD).T] * 2)

    return np.ascontiguousarray(np.concatenate(
        [tiles(w["L0_gnn_bv"]), tiles(w["L0_gnn_bq"]), tiles(w["L0_gnn_bk"]), heads(w["L0_gnn_biq"]),
         heads(w["L0_gnn_bik"]), heads(w["L0_gnn_biv"]), tiles(w["L0_ffn_w1_s"]), tiles(w["L0_ffn_w2_s"]),
         tiles(w["L0_ffn_h1_s"]), tiles(w["L0_ffn_h2_s"])], axis=1))


def kernel(**inputs):
    import numpy as np
    import concourse.bacc as bacc
    from concourse.bass_utils import run_bass_kernel_spmd

    w = {name: np.asarray(a) for name, a in inputs.items()}
    e = [w["src"], w["dst"], w["edge_type_5"]]
    arrays = {
        "x": np.ascontiguousarray(w["x"]),
        "src_dst": np.stack(e[:2]).reshape(2, P, ETILES),
        "edge_cols": np.ascontiguousarray(np.stack(e).reshape(3, ETILES, P).transpose(2, 0, 1)),
        "etw": np.ascontiguousarray(w["L0_gnn_edge_type_weights"]),
        "weights": host_units(w),
        "cols": host_cols(w),
        "bo": np.ascontiguousarray(w["L0_gnn_bo"]),
        "w3_s": np.ascontiguousarray(w["L0_ffn_w3_s"]),
    }
    nc = bacc.Bacc("TRN2", target_bir_lowering=False, num_devices=1)
    args = [nc.dram_tensor(f"in_{n}", a.shape, mybir.dt.from_np(a.dtype), kind="ExternalInput").ap() for n, a in arrays.items()]
    codes = nc.dram_tensor("codes", (EDGES,), F32, kind="Internal").ap()
    out = nc.dram_tensor("out", (NODES, FEAT), F32, kind="ExternalOutput").ap()
    gnn_ffn(nc, *args, codes, out)
    r = run_bass_kernel_spmd(nc, [{f"in_{n}": a for n, a in arrays.items()}], core_ids=[0])
    return r.results[0]["out"]
```

```python
from contextlib import ExitStack

import concourse.bass as bass
from concourse import mybir

F32 = mybir.dt.float32
F32R = mybir.dt.float32r
BF16 = mybir.dt.bfloat16
F16 = mybir.dt.float16
I32 = mybir.dt.int32
ALU = mybir.AluOpType
ACT = mybir.ActivationFunctionType

P = 128
NODES = 384
NT = NODES // P
FEAT = 1024
KT = FEAT // P
HALF = 512
HID = 512
HEADS = 16
HD = FEAT // HEADS
SCALE = 1.0 / 8.0
EDGES = 12288
ETILES = EDGES // P
CHUNKS = ETILES // 2
STEP_BITS = 5
PER_STEP = 4
GROUP = 4 * PER_STEP
EPS = 1e-5
ABSENT = 1e30
ROUNDER = 12582912.0
RING = 4
AHEAD = 3

U_V, U_IV, U_Q, U_K, U_AT, U_WO, U_F1, U_H1, U_H2, U_W3, UNITS = 0, 8, 16, 24, 32, 48, 56, 64, 66, 68, 72
C_BV, C_BQ, C_BK, C_BIQ, C_BIK, C_BIV = 0, 8, 16, 24, 40, 56
C_S1, C_S2, C_H1, C_H2, C_ALL = 72, 76, 80, 84, 88


def gnn_ffn(nc, x_in, src_dst, edge_cols, etw, weights, cols, bo, w3_s, codes_flat, out):
    src_nat, dst_nat = src_dst[0], src_dst[1]
    codes_nat = codes_flat.rearrange("(p f) -> p f", p=P)
    codes = codes_flat.rearrange("(g e) -> g e", g=ETILES // GROUP)
    with ExitStack() as ctx:
        def sem(name):
            return ctx.enter_context(nc.semaphore(name))

        at = [16512]

        def place(name, shape, dt, size):
            t = nc.alloc_sbuf_tensor_at(name, shape, dt, offset=at[0])
            n = size
            for d in shape[1:]:
                n *= d
            at[0] += (n + 31) // 32 * 32
            return t

        stage = place("stage", [P, RING, FEAT], F32, 4)
        w_hi = place("w_hi", [P, RING, FEAT], F32R, 4)
        w_lo = place("w_lo", [P, RING, FEAT], F32R, 4)
        xt_hi = place("xt_hi", [P, KT, NODES], F32R, 4)
        xt_lo = place("xt_lo", [P, KT, NODES], F32R, 4)
        qk_hi = place("qk_hi", [P, 2 * KT, NODES], F32R, 4)
        qk_lo = place("qk_lo", [P, 2 * KT, NODES], F32R, 4)
        keys_end = at[0]
        v2 = place("v2", [P, NT, HEADS, 2 * HD], F32R, 4)
        xs = place("xs", [P, NT, FEAT], F32, 4)
        mask8 = place("mask8", [P, NT, NODES], F32, 4)
        rowvec = place("rowvec", [P, FEAT], F32, 4)
        ident = place("ident", [P, P], F32, 4)
        col = place("col", [P, C_ALL], F32, 4)
        stats = place("stats", [P, NT, 2, 6], F32, 4)
        mv = place("mv", [P, NT, 2], F32, 4)
        ve = place("ve", [P, NT], F32, 4)
        sd = place("sd", [P, NT], F32, 4)
        rstd = place("rstd", [P, NT], F32, 4)
        tmp3 = place("tmp3", [P, NT], F32, 4)
        negmax = place("negmax", [P, 2, NT], F32, 4)
        psums = place("psums", [P, 2, NT], F32, 4)
        rsums = place("rsums", [P, 2, NT], F32, 4)
        w8 = place("w8", [P, 4], F32, 4)
        spx = place("spx", [P, 4, 4], F32, 4)
        shared = at[0]
        keys_room = shared - keys_end + KT * NODES * 4

        xn = place("xn", [P, NT, FEAT], F32, 4)
        rows = place("rows", [P, 2, GROUP * P], F32, 4)
        later = place("later", [P, 256], BF16, 2)
        junk = place("junk", [P, PER_STEP, 256], BF16, 2)
        iota_h = place("iota_h", [P, NODES], F16, 2)
        loops = place("loops", [P, 5 * P], BF16, 2)
        ident_b = place("ident_b", [P, P], BF16, 2)
        ecol = place("ecol", [P, 3, ETILES], F32, 4)
        ecode = place("ecode", [P, ETILES], F32, 4)
        ebase = place("ebase", [P, ETILES], F32, 4)
        cnt = place("cnt", [P, PER_STEP], F32, 4)
        val = place("val", [P, PER_STEP], F32, 4)
        assert at[0] <= nc.sbuf_usable_end, at[0]
        at[0] = shared - keys_room
        oh_src = place("oh_src", [P, 4, NODES], BF16, 2)
        oh_dst = place("oh_dst", [P, 4, NODES], BF16, 2)
        iota_i = place("iota_i", [P, NODES], I32, 4)
        nat_i = place("nat_i", [P, 2, ETILES], I32, 4)
        nat_f = place("nat_f", [P, 2, ETILES], F32, 4)
        ncode = place("ncode", [P, ETILES], F32, 4)
        ecol_i = place("ecol_i", [P, 3, ETILES], I32, 4)
        ebits = place("ebits", [P, ETILES], I32, 4)
        ebase_i = place("ebase_i", [P, ETILES], I32, 4)
        assert at[0] <= shared - keys_room + KT * NODES * 4, at[0]
        at[0] = shared + NT * FEAT * 4
        dec = [place(f"dec{n}", [P, NT, NODES], F32 if n else I32, 4) for n in range(4)]
        at[0] = shared
        q2 = place("q2", [P, 2, 2, NODES], F32R, 4)
        k2_hi = place("k2_hi", [P, 2, 2, NODES], F32R, 4)
        k2_lo = place("k2_lo", [P, 2, 2, NODES], F32R, 4)
        pt_hi = place("pt_hi", [P, NT, NODES], F32R, 4)
        pt_lo = place("pt_lo", [P, NT, NODES], F32R, 4)
        prob = place("prob", [P, 2, NT, NODES], F32, 4)
        pv_t = place("pv_t", [P, NODES], F32, 4)
        pv_u = place("pv_u", [P, NODES], F32, 4)
        assert at[0] <= nc.sbuf_usable_end, at[0]
        at[0] = shared + NT * FEAT * 4
        ffn_g = place("ffn_g", [P, 2, NODES], F32, 4)
        ffn_h = place("ffn_h", [P, 2, NODES], F32, 4)
        yt = place("yt", [P, 2 * NT, HALF], F32, 4)

        bank = [ctx.enter_context(nc.psum_tensor(f"bank{b}", [P, HALF], F32)) for b in range(8)]

        x_sem = [sem(f"x_sem{s}") for s in range(NT)]
        cols_in = sem("cols_in")
        etw_in = sem("etw_in")
        nat_in = sem("nat_in")
        ecol_in = sem("ecol_in")
        bo_in = sem("bo_in")
        w3s_in = sem("w3s_in")
        codes_out = sem("codes_out")
        rows_in = [sem("rows_in0"), sem("rows_in1")]
        w_in = [sem(f"w_in{r}") for r in range(RING)]
        consts = sem("consts")
        hi_ready = sem("hi_ready")
        lo_ready = sem("lo_ready")
        unit_used = sem("unit_used")
        act_hi = sem("act_hi")
        act_lo = sem("act_lo")
        turned = sem("turned")
        ln_dve = sem("ln_dve")
        ln_sd = sem("ln_sd")
        normed = sem("normed")
        tok_done = sem("tok_done")
        v2_hi = sem("v2_hi")
        v2_lo = sem("v2_lo")
        resid = sem("resid")
        xbo = sem("xbo")
        code_nat = sem("code_nat")
        e_ready = sem("e_ready")
        sp_act = sem("sp_act")
        cmp_done = sem("cmp_done")
        val_ready = sem("val_ready")
        onehot = sem("onehot")
        edges_used = sem("edges_used")
        k2_in = [sem("k2_in0"), sem("k2_in1")]
        decoded = sem("decoded")
        k2_act = sem("k2_act")
        k2_ready = sem("k2_ready")
        q2_act = sem("q2_act")
        q2_ready = sem("q2_ready")
        s_done = sem("s_done")
        masked = sem("masked")
        exped = sem("exped")
        rsum = sem("rsum")
        prob_ready = sem("prob_ready")
        scores_seen = sem("scores_seen")
        pt_done = sem("pt_done")
        pt_h = sem("pt_h")
        pt_l = sem("pt_l")
        pv_done = sem("pv_done")
        pv_half = sem("pv_half")
        pv_sum = sem("pv_sum")
        ot_h = sem("ot_h")
        ot_l = sem("ot_l")
        f_act = sem("f_act")
        f_mul = sem("f_mul")
        f_hi = sem("f_hi")
        f_lo = sem("f_lo")
        y_mul = sem("y_mul")
        y_ready = sem("y_ready")
        out_done = sem("out_done")
        st_done = sem("st_done")
        aggr_done = sem("aggr_done")
        src_ready = sem("src_ready")
        h_done = sem("h_done")
        ebase_b = ebase[:].bitcast(I32)

        def f32(ap):
            return ap.bitcast(F32)

        def rows_of(g):
            return codes[g].partition_broadcast(P)

        def ahead(g, uu):
            return RING * g + uu + AHEAD, (uu + AHEAD) % RING, g + 1 + (uu + AHEAD) // RING

        block = ctx.enter_context(nc.Block())

        @block.sync
        def _(sp):
            for s in range(NT):
                sp.dma_start(xs[:, s], x_in[s * P:(s + 1) * P, :]).then_inc(x_sem[s], 16)
            for u in range(RING):
                sp.dma_start(stage[:, u], weights[u]).then_inc(w_in[u], 16)

            def load_group(g, rows_slot):
                for uu in range(RING):
                    sp.wait_ge(lo_ready, RING * g + uu + 1)
                    sp.dma_start(stage[:, uu], weights[RING * g + RING + uu]).then_inc(w_in[uu], 16)
                    if uu == 1 and rows_slot is not None:
                        sp.wait_ge(cmp_done, GROUP * g)
                        sp.dma_start(rows[:, rows_slot], rows_of(g + 1)).then_inc(rows_in[rows_slot], 16)

            load_group(0, None)
            with sp.Fori(0, 2) as i:
                load_group(2 * i + 1, 0)
                load_group(2 * i + 2, 1)
            for g in (5, 6, 7):
                load_group(g, None)

            def copy_keys(j, jb):
                sp.wait_ge(k2_act, 2 * j + 2)
                sp.dma_start(f32(k2_hi[64:128, jb]), f32(k2_hi[0:64, jb])).then_inc(k2_in[jb], 16)
                sp.wait_ge(k2_ready, j + 1)
                sp.dma_start(f32(k2_lo[64:128, jb]), f32(k2_lo[0:64, jb])).then_inc(k2_in[jb], 16)

            def load(g, uu):
                sp.wait_ge(lo_ready, RING * g + uu + 1)
                sp.dma_start(stage[:, uu], weights[RING * g + RING + uu]).then_inc(w_in[uu], 16)

            load(8, 0)
            load(8, 1)
            load(8, 2)
            load(8, 3)
            copy_keys(0, 0)
            load(9, 0)
            load(9, 1)
            copy_keys(1, 1)
            with sp.Fori(0, 3) as i:
                load(9 + i, 2)
                load(9 + i, 3)
                copy_keys(2 * i + 2, 0)
                load(10 + i, 0)
                load(10 + i, 1)
                copy_keys(2 * i + 3, 1)
            load(12, 2)
            load(12, 3)
            with sp.Fori(13, UNITS // RING - 1) as g:
                load_group(g, None)
            sp.wait_ge(xbo, NT)
            sp.dma_start(rowvec[:], w3_s.partition_broadcast(P)).then_inc(w3s_in, 16)
            for n in range(2 * NT):
                h, s = n // NT, n % NT
                sp.wait_ge(y_ready, n + 1)
                sp.dma_start(out[s * P:(s + 1) * P, h * HALF:(h + 1) * HALF], yt[:, n]).then_inc(out_done, 16)
            sp.wait_ge(out_done, 16 * 2 * NT)

        @block.gpsimd
        def _(pool):
            pool.sem_inc(ot_l, 1)
            pool.memset(ident[:], 0.0).then_inc(consts, 1)
            pool.memset(ident_b[:], 0.0).then_inc(consts, 1)
            pool.memset(loops[:], 0.0).then_inc(consts, 1)
            pool.memset(later[:], 1.0).then_inc(consts, 1)
            pool.iota(iota_i[:], pattern=[[1, NODES]], base=0, channel_multiplier=0).then_inc(consts, 1)
            pool.iota(ebase_i[:], pattern=[[STEP_BITS, CHUNKS], [0, 2]], base=7,
                      channel_multiplier=0).then_inc(consts, 1)
            pool.wait_ge(consts, 6)
            pool.affine_select(out=ident[:], in_=ident[:], compare_op=ALU.not_equal, fill=1.0, base=0,
                               pattern=[[-1, P]], channel_multiplier=1).then_inc(consts, 1)
            pool.affine_select(out=ident_b[:], in_=ident_b[:], compare_op=ALU.not_equal, fill=1.0, base=0,
                               pattern=[[-1, P]], channel_multiplier=1).then_inc(consts, 1)
            pool.affine_select(out=loops[:, 2 * P:3 * P], in_=loops[:, 2 * P:3 * P], compare_op=ALU.not_equal,
                               fill=2.0 ** -122, base=0, pattern=[[-1, P]], channel_multiplier=1).then_inc(consts, 1)
            pool.affine_select(out=later[:], in_=later[:], compare_op=ALU.is_gt, fill=0.0, base=0,
                               pattern=[[1, 256]], channel_multiplier=-1).then_inc(consts, 1)
            pool.wait_ge(bo_in, 16)
            for s in range(NT):
                pool.wait_ge(normed, s + 1)
                pool.tensor_tensor(xs[:, s], xs[:, s], rowvec[:], ALU.add).then_inc(xbo, 1)

            def split_ahead(g, uu):
                v, slot, _ = ahead(g, uu)
                pool.wait_ge(hi_ready, v + 1)
                pool.tensor_tensor(w_lo[:, slot], stage[:, slot], f32(w_hi[:, slot]), ALU.subtract).then_inc(lo_ready, 1)

            def attention(i, last):
                for jj in range(2):
                    if not (last and jj == 1):
                        split_ahead(8 + i + jj, (3 + 2 * jj) % RING)
                    if not last:
                        split_ahead(9 + i, 2 * jj)
                    pool.wait_ge(ot_h, 2 * i + jj + 1)
                    pool.tensor_tensor(xt_lo[:, 2 * i + jj], pv_u[:], f32(xt_hi[:, 2 * i + jj]),
                                       ALU.subtract).then_inc(ot_l, 1)

            pool.wait_ge(lo_ready, ahead(8, 3)[0])
            with pool.Fori(0, 3) as i:
                attention(i, False)
            attention(3, True)

        @block.scalar
        def _(act):
            act.dma_start(nat_i[:, 0], src_nat).then_inc(nat_in, 16)
            act.dma_start(nat_i[:, 1], dst_nat).then_inc(nat_in, 16)
            act.dma_start(ecol_i[:], edge_cols).then_inc(ecol_in, 16)
            act.dma_start(col[:], cols).then_inc(cols_in, 16)
            act.dma_start(spx[:, 0], etw.partition_broadcast(P)).then_inc(etw_in, 16)
            act.dma_start(rowvec[:], bo.partition_broadcast(P)).then_inc(bo_in, 16)
            act.wait_ge(code_nat, 1)
            act.dma_start(codes_nat, ncode[:]).then_inc(codes_out, 16)

            def split_hi(v, slot, count):
                act.wait_ge(w_in[slot], 16 * count)
                nc.scalar.activation(w_hi[:, slot], stage[:, slot], ACT.Copy).then_inc(hi_ready, 1)

            def split_ahead(g, uu):
                v, slot, count = ahead(g, uu)
                act.wait_ge(unit_used, v - (RING - 1) + 1)
                split_hi(v, slot, count)

            def layernorm(first):
                act.wait_ge(ln_dve, 1 if first else LN_STEPS + 1)
                nc.scalar.activation(sd[:], ve[:], ACT.Sqrt).then_inc(ln_sd, 1)

            def turned_hi(first):
                for f in range(KT):
                    act.wait_ge(turned, f + 1 + (0 if first else KT))
                    nc.scalar.activation(xt_hi[:, f], bank[2 + f % 2][:, 0:NODES], ACT.Copy).then_inc(act_hi, 1)

            layernorm(True)
            act.wait_ge(e_ready, 4)
            nc.scalar.activation(spx[:, 2], spx[:, 1], ACT.Exp).then_inc(sp_act, 1)
            act.wait_ge(sp_act, 1)
            nc.scalar.activation(spx[:, 3], spx[:, 2], ACT.Ln, bias=1.0).then_inc(sp_act, 1)
            act.wait_ge(codes_out, 16)
            for g in range(2):
                act.dma_start(rows[:, g], rows_of(g)).then_inc(rows_in[g], 16)
            for u in range(AHEAD):
                split_hi(u, u, 1)
            turned_hi(True)
            act.wait_ge(cols_in, 16)

            def project(g, uu, tile, bias):
                act.wait_ge(unit_used, RING * g + uu + 1 + 1)
                nc.scalar.activation(qk_hi[:, tile], bank[uu % 2][:, 0:NODES], ACT.Identity,
                                     bias=col[:, bass.ds(bias, 1)]).then_inc(act_hi, 1)

            with act.Fori(0, 2) as i:
                for uu in range(RING):
                    split_ahead(i, uu)
                    project(i, uu, RING * i + uu, C_BV + RING * i + uu)
            with act.Fori(0, 2) as i:
                for uu in range(RING):
                    split_ahead(i + 2, uu)
                for s in range(NT):
                    if s < NT - 1:
                        act.wait_ge(tok_done, 2 * i + s + 1)
                    else:
                        act.wait_ge(unit_used, U_IV + RING * i + RING + 1)
                    nc.scalar.activation(v2[:, s, bass.ds(8 * i, 8), 0:HD],
                                         bank[2 + s][:].rearrange("p (h d) -> p h d", d=HD),
                                         ACT.Copy).then_inc(v2_hi, 1)
            with act.Fori(0, 4) as i:
                for uu in range(RING):
                    split_ahead(i + 4, uu)
                    project(i + 4, uu, RING * i + uu, C_BQ + RING * i + uu)

            def keys_hi(j, jb):
                act.wait_ge(unit_used, U_AT + 2 * j + 1 + 1)
                for hh in range(2):
                    r = slice(64 * hh, 64 * hh + 64)
                    nc.scalar.activation(k2_hi[0:64, jb, hh], bank[0][r, 0:NODES], ACT.Identity,
                                         bias=col[r, bass.ds(C_BIK + 2 * j + hh, 1)]).then_inc(k2_act, 1)

            def queries_hi(j, jb):
                act.wait_ge(unit_used, U_AT + 2 * j + 2 + 1)
                for hh in range(2):
                    r = slice(64 * hh, 64 * hh + 64)
                    nc.scalar.activation(q2[0:64, jb, hh], bank[1][r, 0:NODES], ACT.Identity,
                                         bias=col[r, bass.ds(C_BIQ + 2 * j + hh, 1)]).then_inc(q2_act, 1)

            def exps(h, hh):
                for s in range(NT):
                    act.wait_ge(masked, 3 * h + s + 1)
                    nc.scalar.activation(prob[:, hh, s], prob[:, hh, s], ACT.Exp, scale=-1.0,
                                         bias=negmax[:, hh, s:s + 1], accum_out=psums[:, hh, s:s + 1]).then_inc(exped, 1)

            def probs_t(h, hh):
                for m in range(NT):
                    act.wait_ge(pt_done, 3 * h + m + 1)
                    nc.scalar.activation(pt_hi[:, m], bank[5 + (3 * hh + m) % 2][:, 0:NODES], ACT.Copy).then_inc(pt_h, 1)

            def head_half(h):
                act.wait_ge(pv_done, h + 1)
                act.wait_ge(pv_sum, h + 1)
                nc.scalar.activation(pv_t[0:64, :], bank[7][64:128, 0:NODES], ACT.Identity,
                                     bias=col[64:128, bass.ds(C_BIV + h, 1)]).then_inc(pv_half, 1)

            def pair_hi(j):
                act.wait_ge(pv_sum, 2 * j + 2 + 1)
                nc.scalar.activation(xt_hi[:, j], pv_u[:], ACT.Copy).then_inc(ot_h, 1)

            split_ahead(8, 0)
            keys_hi(0, 0)
            split_ahead(8, 1)
            queries_hi(0, 0)
            split_ahead(8, 2)
            keys_hi(1, 1)

            def attention(i, last):
                for jj in range(2):
                    a = 4 * i + 2 * jj
                    more = not (last and jj == 1)
                    exps(a, 0)
                    if more:
                        split_ahead(8 + i + jj, (3 + 2 * jj) % RING)
                    probs_t(a, 0)
                    exps(a + 1, 1)
                    if more:
                        queries_hi(2 * i + jj + 1, (jj + 1) % 2)
                    if not last:
                        split_ahead(9 + i, 2 * jj)
                    head_half(a)
                    probs_t(a + 1, 1)
                    if not last:
                        keys_hi(2 * i + jj + 2, jj)
                    head_half(a + 1)
                    pair_hi(2 * i + jj)

            with act.Fori(0, 3) as i:
                attention(i, False)
            attention(3, True)
            for g in (12, 13):
                for uu in range(RING):
                    split_ahead(g, uu)
            layernorm(False)
            turned_hi(False)

            def hidden_hi(n, tile):
                act.wait_ge(f_mul, n + 1) if n < 4 else act.wait_ge(f_act, n + 1)
                src = ffn_h if n < 4 else ffn_g
                nc.scalar.activation(qk_hi[:, tile], src[:, n % 2], ACT.Copy).then_inc(f_hi, 1)

            for j in range(4):
                split_ahead(14 + j // 2, 2 * (j % 2))
                act.wait_ge(unit_used, U_F1 + 2 * j + 1 + 1)
                if j >= 2:
                    act.wait_ge(f_mul, j - 1)
                nc.scalar.activation(ffn_g[:, j % 2], bank[2 * (j % 2)][:, 0:NODES], ACT.Silu,
                                     scale=col[:, C_S1 + j:C_S1 + j + 1]).then_inc(f_act, 1)
                split_ahead(14 + j // 2, 2 * (j % 2) + 1)
                hidden_hi(j, j)
            for n in range(4, 12):
                layer, o = (n - 4) // 4, n % 4
                if n % 2 == 0 and n // 2 - 2 + U_H1 + AHEAD < UNITS:
                    split_ahead(16, n // 2 - 2)
                act.wait_ge(h_done, n - 3)
                act.wait_ge(f_lo, n - 1)
                nc.scalar.activation(ffn_g[:, n % 2], bank[n % 4][:, 0:NODES], ACT.Gelu,
                                     scale=col[:, C_H1 + n - 4:C_H1 + n - 3]).then_inc(f_act, 1)
                hidden_hi(n, n)
            split_ahead(17, 0)

        @block.vector
        def _(dve):
            for counted in (v2_lo, pv_sum, resid):
                dve.sem_inc(counted, 1)

            def split_lo(v, slot):
                dve.wait_ge(hi_ready, v + 1)
                nc.vector.tensor_tensor(w_lo[:, slot], stage[:, slot], f32(w_hi[:, slot]),
                                        ALU.subtract).then_inc(lo_ready, 1)

            def split_ahead(g, uu):
                v, slot, _ = ahead(g, uu)
                split_lo(v, slot)

            links = [0]

            def link(ins, signal):
                links[0] += 1
                ins.then_inc(signal, 1)
                dve.wait_ge(signal, links[0])

            def stats_of(s, hf):
                return nc.vector.bn_stats(stats[:, s, hf], xs[:, s, hf * HALF:(hf + 1) * HALF])

            def layernorm(first, done):
                links[0] = 0 if first else LN_STEPS
                for s in range(NT):
                    last = nc.vector.bn_aggr(mv[:, s], stats[:, s].rearrange("p a b -> p (a b)"))
                last.then_inc(done, 1)
                dve.wait_ge(done, 1 if first else 2)
                link(nc.vector.tensor_scalar(ve[:], mv[:, :, 1], EPS, None, ALU.add), ln_dve)
                dve.wait_ge(ln_sd, 1 if first else 2)
                link(nc.vector.reciprocal(rstd[:], sd[:]), ln_dve)
                link(nc.vector.tensor_tensor(tmp3[:], rstd[:], rstd[:], ALU.mult), ln_dve)
                link(nc.vector.tensor_tensor(tmp3[:], tmp3[:], ve[:], ALU.mult), ln_dve)
                link(nc.vector.tensor_scalar(tmp3[:], tmp3[:], -0.5, 1.5, ALU.mult, ALU.add), ln_dve)
                link(nc.vector.tensor_tensor(rstd[:], rstd[:], tmp3[:], ALU.mult), ln_dve)
                for s in range(NT):
                    nc.vector.tensor_scalar(xn[:, s], xs[:, s], mv[:, s, 0:1], rstd[:, s:s + 1],
                                            ALU.subtract, ALU.mult).then_inc(normed, 1)

            def turned_lo(first):
                for f in range(KT):
                    dve.wait_ge(act_hi, f + 1 + (0 if first else 32))
                    nc.vector.tensor_tensor(xt_lo[:, f], bank[2 + f % 2][:, 0:NODES], f32(xt_hi[:, f]),
                                            ALU.subtract).then_inc(act_lo, 1)

            dve.wait_ge(nat_in, 32)
            nc.vector.tensor_copy(nat_f[:], nat_i[:]).then_inc(e_ready, 1)
            dve.wait_ge(e_ready, 1)
            nc.vector.scalar_tensor_tensor(out=ncode[:], in0=nat_f[:, 0], scalar=float(NODES), in1=nat_f[:, 1],
                                           op0=ALU.mult, op1=ALU.add).then_inc(code_nat, 1)
            for s in range(NT):
                dve.wait_ge(x_sem[s], 16)
                for hf in range(2):
                    last = stats_of(s, hf)
            last.then_inc(st_done, 1)
            dve.wait_ge(st_done, 1)
            layernorm(True, aggr_done)
            dve.wait_ge(ecol_in, 16)
            nc.vector.tensor_copy(ecol[:], ecol_i[:]).then_inc(e_ready, 1)
            dve.wait_ge(etw_in, 16)
            nc.vector.tensor_scalar(spx[:, 1], spx[:, 0], -1.0, None, ALU.mult).then_inc(e_ready, 1)
            dve.wait_ge(e_ready, 3)
            nc.vector.tensor_tensor(spx[:, 1], spx[:, 1], spx[:, 0], ALU.min).then_inc(e_ready, 1)
            nc.vector.scalar_tensor_tensor(out=ecode[:], in0=ecol[:, 0], scalar=float(NODES), in1=ecol[:, 1],
                                           op0=ALU.mult, op1=ALU.add).then_inc(e_ready, 1)
            nc.vector.tensor_scalar(ebase[:], ecol[:, 2], 0.0, 4.0, ALU.is_equal, ALU.mult).then_inc(e_ready, 1)
            dve.wait_ge(e_ready, 6)
            nc.vector.scalar_tensor_tensor(out=ebase[:], in0=ecol[:, 2], scalar=-1.0, in1=ebase[:],
                                           op0=ALU.add, op1=ALU.add).then_inc(e_ready, 1)
            dve.wait_ge(e_ready, 7)
            dve.wait_ge(consts, 10)
            nc.vector.tensor_tensor(ebits[:], ebase[:], ebase_i[:], ALU.add).then_inc(e_ready, 1)
            nc.vector.tensor_copy(iota_h[:], iota_i[:]).then_inc(e_ready, 1)
            dve.wait_ge(e_ready, 9)
            nc.vector.tensor_scalar(ebase_b, ebits[:], 23, None, ALU.logical_shift_left).then_inc(e_ready, 1)
            dve.wait_ge(e_ready, 10)
            for u in range(AHEAD):
                split_lo(u, u)
            turned_lo(True)
            dve.wait_ge(cols_in, 16)

            def edge_step(g, uu, slot):
                t0 = GROUP * g + PER_STEP * uu
                for d in range(PER_STEP):
                    tl = PER_STEP * uu + d
                    lo = 256 * (tl // 2) + P * (tl % 2)
                    w = 256 - P * (tl % 2)
                    nc.vector.scalar_tensor_tensor(
                        out=junk[:, d, 0:w], in0=rows[:, slot, lo:lo + w], scalar=ecode[:, bass.ds(t0 + d, 1)],
                        in1=later[:, 0:w], op0=ALU.is_equal, op1=ALU.mult, accum_out=cnt[:, d:d + 1]).then_inc(cmp_done, 1)
                for d in range(PER_STEP):
                    dve.wait_ge(edges_used, t0 + d + 1)
                    nc.vector.tensor_scalar(oh_src[:, d], iota_h[:], ecol[:, 0, bass.ds(t0 + d, 1)], None,
                                            ALU.is_equal).then_inc(src_ready, 1)
                    if d == 0:
                        dve.wait_ge(cmp_done, t0 + PER_STEP)
                        nc.vector.scalar_tensor_tensor(
                            out=val[:], in0=cnt[:], scalar=0.0, in1=ebase[:, bass.ds(t0, PER_STEP)],
                            op0=ALU.is_equal, op1=ALU.mult).then_inc(val_ready, 1)
                for d in range(PER_STEP):
                    if d == 0:
                        dve.wait_ge(val_ready, RING * g + uu + 1)
                    nc.vector.tensor_scalar(oh_dst[:, d], iota_h[:], ecol[:, 1, bass.ds(t0 + d, 1)],
                                            val[:, d:d + 1], ALU.is_equal, ALU.mult).then_inc(onehot, 1)

            def rows_wait(slot, count):
                dve.wait_ge(rows_in[slot], 16 * count)

            def project_lo(n, uu, tile, bias):
                dve.wait_ge(act_hi, KT + n + 1)
                nc.vector.scalar_tensor_tensor(
                    out=qk_lo[:, tile], in0=bank[uu % 2][:, 0:NODES], scalar=col[:, bass.ds(bias, 1)],
                    in1=f32(qk_hi[:, tile]), op0=ALU.add, op1=ALU.subtract).then_inc(act_lo, 1)

            for g in range(2):
                rows_wait(g, 1)
                for uu in range(RING):
                    split_ahead(g, uu)
                    edge_step(g, uu, g)
                    project_lo(RING * g + uu, uu, RING * g + uu, C_BV + RING * g + uu)
            for g in range(2, 4):
                rows_wait(g % 2, 2)
                for uu in range(RING):
                    split_ahead(g, uu)
                    edge_step(g, uu, g % 2)
                for s in range(NT):
                    n = NT * (g - 2) + s
                    dve.wait_ge(v2_hi, n + 1)
                    heads = slice(8 * (g - 2), 8 * (g - 2) + 8)
                    nc.vector.tensor_tensor(v2[:, s, heads, HD:2 * HD], bank[2 + s][:].rearrange("p (h d) -> p h d", d=HD),
                                            f32(v2[:, s, heads, 0:HD]), ALU.subtract).then_inc(v2_lo, 1)
            for g in (4, 5):
                rows_wait(g % 2, 3)
                for uu in range(RING):
                    split_ahead(g, uu)
                    edge_step(g, uu, g % 2)
                    n = RING * (g - 4) + uu
                    project_lo(KT + n, uu, n, C_BQ + n)

            d_i, d_e, d_q, d_m = dec
            links[0] = 0

            def decode(part):
                if part == 0:
                    dve.wait_ge(edges_used, ETILES + 3 + 1)
                    dve.wait_ge(sp_act, 2)
                    link(nc.vector.scalar_tensor_tensor(out=w8[:], in0=spx[:, 0], scalar=0.0, in1=spx[:, 3],
                                                        op0=ALU.max, op1=ALU.add), decoded)
                    link(nc.vector.tensor_scalar(w8[:], w8[:], 8.0, None, ALU.mult), decoded)
                    for s in range(NT):
                        links[0] += 1
                        nc.vector.tensor_copy(d_m[:, s], bank[5 + s][:, 0:NODES]).then_inc(decoded, 1)
                    dve.wait_ge(decoded, links[0])
                elif part == 1:
                    link(nc.vector.tensor_scalar(d_i[:], d_m[:].bitcast(I32), 23, None, ALU.logical_shift_right), decoded)
                    link(nc.vector.tensor_scalar(mask8[:], d_m[:], 0.0, 1.0, ALU.is_gt, ALU.subtract), decoded)
                elif part == 2:
                    link(nc.vector.tensor_copy(d_e[:], d_i[:]), decoded)
                    link(nc.vector.tensor_scalar(d_q[:], d_e[:], 0.2, -0.8, ALU.mult, ALU.add), decoded)
                    link(nc.vector.tensor_scalar(d_q[:], d_q[:], ROUNDER, ROUNDER, ALU.add, ALU.subtract), decoded)
                elif part == 3:
                    link(nc.vector.scalar_tensor_tensor(out=d_e[:], in0=d_q[:], scalar=-5.0, in1=d_e[:],
                                                        op0=ALU.mult, op1=ALU.add), decoded)
                    link(nc.vector.tensor_scalar(d_m[:], d_e[:], 2.0, w8[:, 0:1], ALU.is_equal, ALU.mult), decoded)
                elif part < 7:
                    n = part - 3
                    link(nc.vector.tensor_scalar(d_q[:], d_e[:], float(n + 2), w8[:, n:n + 1], ALU.is_equal, ALU.mult), decoded)
                    link(nc.vector.tensor_tensor(d_m[:], d_m[:], d_q[:], ALU.add), decoded)
                else:
                    link(nc.vector.scalar_tensor_tensor(out=mask8[:], in0=mask8[:], scalar=ABSENT, in1=d_m[:],
                                                        op0=ALU.mult, op1=ALU.add), decoded)

            for n in range(KT):
                split_ahead(6 + n // RING, n % RING)
                decode(n)
                project_lo(2 * KT + n, n % 2, KT + n, C_BK + n)

            def keys_lo(j, jb):
                dve.wait_ge(k2_act, 2 * j + 2)
                for hh in range(2):
                    last = nc.vector.scalar_tensor_tensor(
                        out=k2_lo[0:64, jb, hh], in0=bank[0][64 * hh:64 * hh + 64, 0:NODES],
                        scalar=col[0:64, bass.ds(C_BIK + 2 * j + hh, 1)], in1=f32(k2_hi[0:64, jb, hh]),
                        op0=ALU.add, op1=ALU.subtract)
                last.then_inc(k2_ready, 1)

            def queries_lo(j, jb):
                dve.wait_ge(q2_act, 2 * j + 2)
                for hh in range(2):
                    r = slice(64 * hh, 64 * hh + 64)
                    last = nc.vector.scalar_tensor_tensor(
                        out=q2[64:128, jb, hh], in0=bank[1][r, 0:NODES],
                        scalar=col[0:64, bass.ds(C_BIQ + 2 * j + hh, 1)], in1=f32(q2[0:64, jb, hh]),
                        op0=ALU.add, op1=ALU.subtract)
                last.then_inc(q2_ready, 1)

            def mask_scores(h, hh, s):
                dve.wait_ge(s_done, 3 * h + s + 1)
                dve.sem_inc(scores_seen, 1)
                nc.vector.tensor_tensor_reduce(prob[:, hh, s], bank[2 + s][:, 0:NODES], mask8[:, s], -SCALE, 3e38,
                                               ALU.add, ALU.min, negmax[:, hh, s:s + 1]).then_inc(masked, 1)

            def normalise(h, hh):
                for s in range(NT + 1):
                    if s < NT:
                        dve.wait_ge(exped, 3 * h + s + 1)
                        nc.vector.reciprocal(rsums[:, hh, s:s + 1], psums[:, hh, s:s + 1]).then_inc(rsum, 1)
                    if s > 0:
                        dve.wait_ge(rsum, 3 * h + s)
                        nc.vector.tensor_scalar(prob[:, hh, s - 1], prob[:, hh, s - 1], rsums[:, hh, s - 1:s], None,
                                                ALU.mult).then_inc(prob_ready, 1)

            def probs_lo(h, hh, m):
                dve.wait_ge(pt_h, 3 * h + m + 1)
                nc.vector.tensor_tensor(pt_lo[:, m], bank[5 + (3 * hh + m) % 2][:, 0:NODES], f32(pt_hi[:, m]),
                                        ALU.subtract).then_inc(pt_l, 1)

            def head_sum(h, hh, j):
                r = slice(64 * hh, 64 * hh + 64)
                dve.wait_ge(pv_half, h + 1)
                dve.wait_ge(ot_l, j + 1)
                nc.vector.tensor_tensor(pv_u[r, :], bank[7][0:64, 0:NODES], pv_t[0:64, :], ALU.add).then_inc(pv_sum, 1)

            split_ahead(8, 0)
            keys_lo(0, 0)
            split_ahead(8, 1)
            queries_lo(0, 0)
            split_ahead(8, 2)
            keys_lo(1, 1)

            def attention(i, last):
                for jj in range(2):
                    j = 2 * i + jj
                    a, b = 4 * i + 2 * jj, 4 * i + 2 * jj + 1
                    for s in range(NT):
                        mask_scores(a, 0, s)
                    normalise(a, 0)
                    probs_lo(a, 0, 0)
                    probs_lo(a, 0, 1)
                    mask_scores(b, 1, 0)
                    probs_lo(a, 0, 2)
                    mask_scores(b, 1, 1)
                    mask_scores(b, 1, 2)
                    normalise(b, 1)
                    if not (last and jj == 1):
                        queries_lo(j + 1, (jj + 1) % 2)
                    head_sum(a, 0, j)
                    for m in range(NT):
                        probs_lo(b, 1, m)
                    if not last:
                        keys_lo(j + 2, jj)
                    head_sum(b, 1, j)

            with dve.Fori(0, 3) as i:
                attention(i, False)
            attention(3, True)
            dve.wait_ge(lo_ready, ahead(12, 0)[0])
            for h in range(2):
                for uu in range(RING):
                    split_ahead(12 + h, uu)
                dve.wait_ge(xbo, NT)
                for s in range(NT):
                    if s < NT - 1:
                        dve.wait_ge(tok_done, 4 + 2 * h + s + 1)
                    else:
                        dve.wait_ge(unit_used, U_WO + RING * h + RING + 1)
                    xh = xs[:, s, h * HALF:(h + 1) * HALF]
                    nc.vector.tensor_tensor(xh, bank[2 + s][:], xh, ALU.add).then_inc(resid, 1)
                dve.wait_ge(resid, NT * h + NT + 1)
                for s in range(NT):
                    last = stats_of(s, h)
            last.then_inc(st_done, 1)
            dve.wait_ge(st_done, 2)
            layernorm(False, aggr_done)
            turned_lo(False)

            def hidden_lo(n):
                src = ffn_h if n < 4 else ffn_g
                dve.wait_ge(f_hi, n + 1)
                nc.vector.tensor_tensor(qk_lo[:, n], src[:, n % 2], f32(qk_hi[:, n]), ALU.subtract).then_inc(f_lo, 1)

            for j in range(4):
                split_ahead(14 + j // 2, 2 * (j % 2))
                split_ahead(14 + j // 2, 2 * (j % 2) + 1)
                dve.wait_ge(f_act, j + 1)
                dve.wait_ge(unit_used, U_F1 + 2 * j + 2 + 1)
                nc.vector.scalar_tensor_tensor(out=ffn_h[:, j % 2], in0=bank[2 * (j % 2) + 1][:, 0:NODES],
                                               scalar=col[:, C_S2 + j:C_S2 + j + 1], in1=ffn_g[:, j % 2],
                                               op0=ALU.mult, op1=ALU.mult).then_inc(f_mul, 1)
                hidden_lo(j)
            for n in range(4, 12):
                if n % 2 == 0 and n // 2 - 2 + U_H1 + AHEAD < UNITS:
                    split_ahead(16, n // 2 - 2)
                hidden_lo(n)
            split_ahead(17, 0)
            dve.wait_ge(w3s_in, 16)
            for n in range(2 * NT):
                h, s = n // NT, n % NT
                if s < NT - 1:
                    dve.wait_ge(tok_done, 8 + 2 * h + s + 1)
                else:
                    dve.wait_ge(unit_used, U_W3 + 2 * h + 2 + 1)
                nc.vector.tensor_tensor(yt[:, n], bank[2 + 3 * h + s][:], rowvec[:, h * HALF:(h + 1) * HALF],
                                        ALU.mult).then_inc(y_mul, 1)
                dve.wait_ge(y_mul, n + 1)
                nc.vector.tensor_tensor(yt[:, n], yt[:, n], xs[:, s, h * HALF:(h + 1) * HALF], ALU.add).then_inc(y_ready, 1)

        @block.tensor
        def _(pe):
            pe.sem_inc(unit_used, 1)
            pe.sem_inc(edges_used, 1)

            def turn(first):
                for f in range(KT):
                    if first and f >= 2:
                        pe.wait_ge(act_lo, f - 1)
                    if not first:
                        pe.wait_ge(act_lo, 32 + f - 1)
                    for s in range(NT):
                        if f == 0:
                            pe.wait_ge(normed, s + 1 + (0 if first else NT))
                        last = nc.tensor.transpose(bank[2 + f % 2][:, s * P:(s + 1) * P], xn[:, s, f * P:(f + 1) * P], ident[:])
                    last.then_inc(turned, 1)

            def by_weight(slot, offset, kt, acts, a0, dst, passes, tail=None):
                n, last_n = 0, 3 * kt - 1
                for k in range(kt):
                    w = slice(offset + k * P, offset + (k + 1) * P)
                    for wp, ap in ((w_hi, acts[0]), (w_hi, acts[1]), (w_lo, acts[0])):
                        if passes[0] <= n < passes[1]:
                            last = nc.tensor.matmul(dst[:, 0:NODES], wp[:, slot, w], ap[:, a0 + k], start=n == 0, stop=n == last_n)
                        n += 1
                return last

            ALLP = (0, 24)
            XT, QK = (xt_hi, xt_lo), (qk_hi, qk_lo)

            def by_nodes(slot, pair, pairs, acts, a0, banks, done, wait_bank):
                for s in range(NT):
                    wait_bank(s)
                    for k2 in range(2):
                        k = 2 * pair + k2
                        a = slice(s * P, (s + 1) * P)
                        c = slice(k2 * HALF, (k2 + 1) * HALF)
                        for m, (ap, wp) in enumerate(((acts[0], w_hi), (acts[0], w_lo), (acts[1], w_hi))):
                            last = nc.tensor.matmul(banks[s][:], ap[:, a0 + k, a], wp[:, slot, c],
                                                    start=k == 0 and m == 0, stop=k == 2 * pairs - 1 and m == 2)
                    if pair == pairs - 1 and s < NT - 1:
                        last.then_inc(done, 1)
                last.then_inc(unit_used, 1)

            def edges(g, uu):
                for e in range(PER_STEP):
                    pe.wait_ge(onehot, GROUP * g + PER_STEP * uu + e + 1)
                    for s in range(NT):
                        last = nc.tensor.matmul(bank[5 + s][:, 0:NODES], oh_src[:, e, s * P:(s + 1) * P], oh_dst[:, e],
                                                start=False, stop=True, skip_group_check=True)
                    last.then_inc(edges_used, 1)

            pe.wait_ge(consts, 10)
            turn(True)
            for s in range(NT):
                nc.tensor.matmul(bank[5 + s][:, 0:NODES], ident_b[:], loops[:, 2 * P - s * P:2 * P - s * P + NODES],
                                 start=True, stop=True, skip_group_check=True).then_inc(edges_used, 1)

            def project(g, uu, n):
                pe.wait_ge(lo_ready, RING * g + uu + 1)
                pe.wait_ge(act_lo, KT + n - 1)
                by_weight(uu, 0, KT, XT, 0, bank[uu % 2], ALLP).then_inc(unit_used, 1)

            pe.wait_ge(act_lo, KT)
            with pe.Fori(0, 2) as i:
                for uu in range(RING):
                    project(i, uu, RING * i + uu)
                    edges(i, uu)
            pe.wait_ge(act_lo, 2 * KT)
            with pe.Fori(0, 2) as i:
                for uu in range(RING):
                    pe.wait_ge(lo_ready, U_IV + RING * i + uu + 1)
                    by_nodes(uu, uu, RING, QK, 0, bank[2:5], tok_done,
                             lambda s: pe.wait_ge(v2_lo, NT * i + 1) if uu == 0 and s == 0 else None)
                    edges(i + 2, uu)
            with pe.Fori(0, 2) as i:
                for uu in range(RING):
                    project(i + 4, uu, KT + RING * i + uu)
                    edges(i + 4, uu)
            with pe.Fori(0, 2) as i:
                for uu in range(RING):
                    project(i + 6, uu, 2 * KT + RING * i + uu)

            pe.wait_ge(act_lo, 4 * KT)

            def inner(u, b, parts, ready, j):
                if parts[0] == 0:
                    pe.wait_ge(lo_ready, u + 1)
                    pe.wait_ge(ready, j)
                last = by_weight(u % RING, 0, KT, QK, KT * (1 - b), bank[b], parts)
                if parts[1] == 24:
                    last.then_inc(unit_used, 1)

            def scores(h, s):
                j = h // 2
                if s == 0:
                    pe.wait_ge(k2_in[j % 2], 32 * (j // 2 + 1))
                    pe.wait_ge(q2_ready, j + 1)
                if h:
                    pe.wait_ge(masked, 3 * h + s - 2)
                for n, k2 in enumerate((k2_hi, k2_lo)):
                    last = nc.tensor.matmul(bank[2 + s][:, 0:NODES], q2[:, j % 2, h % 2, s * P:(s + 1) * P], k2[:, j % 2, h % 2],
                                            start=n == 0, stop=n == 1)
                last.then_inc(s_done, 1)

            def turn_probs(h, m):
                if m == 0:
                    pe.wait_ge(prob_ready, 3 * h + 3)
                if 3 * h + m >= 2:
                    pe.wait_ge(pt_l, 3 * h + m - 1)
                for s in range(NT):
                    last = nc.tensor.transpose(bank[5 + (3 * (h % 2) + m) % 2][:, s * P:(s + 1) * P],
                                               prob[:, h % 2, s, m * P:(m + 1) * P], ident[:])
                last.then_inc(pt_done, 1)

            def weigh(h):
                pe.wait_ge(pv_sum, h + 1)
                for m in range(NT):
                    pe.wait_ge(pt_l, 3 * h + m + 1)
                    for n, pt in enumerate((pt_hi, pt_lo)):
                        last = nc.tensor.matmul(bank[7][:, 0:NODES], v2[:, m, h], pt[:, m],
                                                start=m == 0 and n == 0, stop=m == NT - 1 and n == 1)
                last.then_inc(pv_done, 1)

            pairs = HEADS // 2
            inner(U_AT, 0, (0, 24), k2_ready, 0)
            inner(U_AT + 1, 1, (0, 24), q2_ready, 0)
            inner(U_AT + 2, 0, (0, 24), k2_ready, 1)
            for j in range(pairs):
                a, b = 2 * j, 2 * j + 1
                for s in range(NT):
                    scores(a, s)
                if j + 1 < pairs:
                    inner(U_AT + 2 * j + 3, 1, (0, 24), q2_ready, j + 1)
                turn_probs(a, 0)
                turn_probs(a, 1)
                scores(b, 0)
                turn_probs(a, 2)
                scores(b, 1)
                scores(b, 2)
                if j + 2 < pairs:
                    inner(U_AT + 2 * j + 4, 0, (0, 18), k2_ready, j + 2)
                weigh(a)
                for m in range(NT):
                    turn_probs(b, m)
                if j + 2 < pairs:
                    inner(U_AT + 2 * j + 4, 0, (18, 24), k2_ready, j + 2)
                weigh(b)

            with pe.Fori(0, 2) as i:
                for uu in range(RING):
                    pe.wait_ge(lo_ready, U_WO + RING * i + uu + 1)
                    pe.wait_ge(ot_l, 2 * uu + 2 + 1)
                    by_nodes(uu, uu, RING, XT, 0, bank[2:5], tok_done,
                             lambda s: pe.wait_ge(resid, NT * i + 1) if uu == 0 and s == 0 else None)
            turn(False)
            pe.wait_ge(act_lo, 5 * KT)
            for j in range(4):
                for n in range(2):
                    u = U_F1 + 2 * j + n
                    pe.wait_ge(lo_ready, u + 1)
                    if j >= 2:
                        pe.wait_ge(f_mul, j - 1)
                    by_weight(u % RING, 0, KT, XT, 0, bank[2 * (j % 2) + n], ALLP).then_inc(unit_used, 1)
            for n in range(4, 12):
                u = U_H1 + (n - 4) // 2
                pe.wait_ge(lo_ready, u + 1)
                pe.wait_ge(f_lo, 4 if n < 8 else 8)
                last = by_weight(u % RING, HALF * (n % 2), 4, QK, 0 if n < 8 else 4, bank[n % 4], ALLP)
                last.then_inc(h_done, 1)
                if n % 2 == 1:
                    pe.wait_ge(h_done, n - 3)
                    pe.nop().then_inc(unit_used, 1)
            for h in range(2):
                for pair in range(2):
                    u = U_W3 + 2 * h + pair
                    pe.wait_ge(lo_ready, u + 1)
                    pe.wait_ge(f_lo, 12)
                    by_nodes(u % RING, pair, 2, QK, 8, bank[2 + 3 * h:5 + 3 * h], tok_done, lambda s: None)


LN_STEPS = 6


def host_units(w):
    import numpy as np

    def by_weight(a):
        o, i = a.shape
        per = FEAT // i
        return a.reshape(o // P // per, per, P, i // P, P).transpose(0, 4, 1, 3, 2).reshape(-1, P, FEAT)

    def by_nodes(a):
        o, i = a.shape
        return a.reshape(o // HALF, HALF, i // (2 * P), 2, P).transpose(0, 2, 4, 3, 1).reshape(-1, P, FEAT)

    def in_turn(a, b):
        return np.stack([by_weight(a), by_weight(b)], axis=1).reshape(-1, P, FEAT)

    units = [by_weight(w["L0_gnn_wv"]), by_nodes(w["L0_gnn_wiv"]), by_weight(w["L0_gnn_wq"]), by_weight(w["L0_gnn_wk"]),
             in_turn(w["L0_gnn_wik"], w["L0_gnn_wiq"]), by_nodes(w["L0_gnn_wo"]), in_turn(w["L0_ffn_w1_w"], w["L0_ffn_w2_w"]),
             by_weight(w["L0_ffn_h1_w"]), by_weight(w["L0_ffn_h2_w"]), by_nodes(w["L0_ffn_w3_w"])]
    return np.ascontiguousarray(np.concatenate(units))


def host_cols(w):
    import numpy as np

    def tiles(a):
        return a.reshape(-1, P).T

    def heads(a):
        return np.concatenate([a.reshape(HEADS, HD).T] * 2)

    return np.ascontiguousarray(np.concatenate(
        [tiles(w["L0_gnn_bv"]), tiles(w["L0_gnn_bq"]), tiles(w["L0_gnn_bk"]), heads(w["L0_gnn_biq"]),
         heads(w["L0_gnn_bik"]), heads(w["L0_gnn_biv"]), tiles(w["L0_ffn_w1_s"]), tiles(w["L0_ffn_w2_s"]),
         tiles(w["L0_ffn_h1_s"]), tiles(w["L0_ffn_h2_s"])], axis=1))


def kernel(**inputs):
    import numpy as np
    import concourse.bacc as bacc
    from concourse.bass_utils import run_bass_kernel_spmd

    w = {name: np.asarray(a) for name, a in inputs.items()}
    e = [w["src"], w["dst"], w["edge_type_5"]]
    arrays = {
        "x": np.ascontiguousarray(w["x"]),
        "src_dst": np.stack(e[:2]).reshape(2, P, ETILES),
        "edge_cols": np.ascontiguousarray(np.stack(e).reshape(3, ETILES, P).transpose(2, 0, 1)),
        "etw": np.ascontiguousarray(w["L0_gnn_edge_type_weights"]),
        "weights": host_units(w),
        "cols": host_cols(w),
        "bo": np.ascontiguousarray(w["L0_gnn_bo"]),
        "w3_s": np.ascontiguousarray(w["L0_ffn_w3_s"]),
    }
    nc = bacc.Bacc("TRN2", target_bir_lowering=False, num_devices=1)
    args = [nc.dram_tensor(f"in_{n}", a.shape, mybir.dt.from_np(a.dtype), kind="ExternalInput").ap() for n, a in arrays.items()]
    codes = nc.dram_tensor("codes", (EDGES,), F32, kind="Internal").ap()
    out = nc.dram_tensor("out", (NODES, FEAT), F32, kind="ExternalOutput").ap()
    gnn_ffn(nc, *args, codes, out)
    r = run_bass_kernel_spmd(nc, [{f"in_{n}": a for n, a in arrays.items()}], core_ids=[0])
    return r.results[0]["out"]
```

```python
from contextlib import ExitStack

import concourse.bass as bass
from concourse import mybir

F32 = mybir.dt.float32
F32R = mybir.dt.float32r
BF16 = mybir.dt.bfloat16
I32 = mybir.dt.int32
ALU = mybir.AluOpType
ACT = mybir.ActivationFunctionType

P = 128
NODES = 384
NT = NODES // P
FEAT = 1024
KT = FEAT // P
HALF = 512
HEADS = 16
HD = FEAT // HEADS
SCALE = 1.0 / 8.0
EDGES = 12288
ETILES = EDGES // P
PER_UNIT = 3
WINDOW = 4
GROUP = 16
GROUP_COLS = (GROUP + WINDOW - 1) * P
CELLS = NODES * NODES
EPS = 1e-5
ABSENT = 1e30
RING = 4
AHEAD = 3
PROB_BANKS = ((5, 6, 2), (4, 5, 6))
V2_BANKS = ((4, 5, 6), (7, 2, 3))
TURN_BANKS = (0, 1, 2, 6, 7, 3, 4, 5)

U_IV, U_Q, U_AT, U_WO, U_F1, U_H1, U_W3, UNITS = 8, 16, 32, 48, 56, 64, 68, 72
FFN_UNITS = UNITS - U_F1
C_BV, C_BQ, C_BK, C_BIQ, C_BIK, C_BIV = 0, 8, 16, 24, 40, 56
C_S1, C_S2, C_H1, C_H2, C_ALL = 72, 76, 80, 84, 88

WARM_UP = 30
LN_STEPS = (6, 6, 5)


def gnn_ffn(nc, x_in, src_dst, edge_cols, etw, weights, cols, bo, w3_s, codes_flat, table, out):
    codes_nat = codes_flat.rearrange("(p f) -> p f", p=P)
    table_nat = table[0:CELLS].rearrange("(s p m) one -> p s (m one)", p=P, m=NODES)
    with ExitStack() as ctx:
        def sem(name):
            return ctx.enter_context(nc.semaphore(name))

        at = [16512]

        def place(name, shape, dt, size):
            t = nc.alloc_sbuf_tensor_at(name, shape, dt, offset=at[0])
            n = size
            for d in shape[1:]:
                n *= d
            at[0] += (n + 31) // 32 * 32
            return t

        stage = place("stage", [P, RING, FEAT], F32, 4)
        w_hi = place("w_hi", [P, RING, FEAT], F32R, 4)
        w_lo = place("w_lo", [P, RING, FEAT], F32R, 4)
        xt_hi = place("xt_hi", [P, KT, NODES], F32R, 4)
        xt_lo = place("xt_lo", [P, KT, NODES], F32R, 4)
        qk_hi = place("qk_hi", [P, 2 * KT, NODES], F32R, 4)
        qk_lo = place("qk_lo", [P, 2 * KT, NODES], F32R, 4)
        keys_end = at[0]
        v2 = place("v2", [P, NT, HEADS, 2 * HD], F32R, 4)
        xs = place("xs", [P, NT, FEAT], F32, 4)
        mask8 = place("mask8", [P, NT, NODES], F32, 4)
        rowvec = place("rowvec", [P, FEAT], F32, 4)
        ident = place("ident", [P, P], F32, 4)
        col = place("col", [P, C_ALL], F32, 4)
        stats = place("stats", [P, NT, 2, 6], F32, 4)
        mv = place("mv", [P, NT, 2], F32, 4)
        ve = place("ve", [P, NT], F32, 4)
        sd = place("sd", [P, NT], F32, 4)
        rstd = place("rstd", [P, NT], F32, 4)
        shift = place("shift", [P, 2], F32, 4)
        tmp3 = place("tmp3", [P, NT], F32, 4)
        negmax = place("negmax", [P, 2, NT], F32, 4)
        psums = place("psums", [P, 2, NT], F32, 4)
        rsums = place("rsums", [P, 2, NT], F32, 4)
        w8 = place("w8", [P, 4], F32, 4)
        spx = place("spx", [P, 4, 4], F32, 4)
        ones = place("ones", [P, 1], F32, 4)
        inexact = place("inexact", [P, FFN_UNITS], F32, 4)
        flags = place("flags", [P, FFN_UNITS], I32, 4)
        shared = at[0]

        xn = place("xn", [P, NT, FEAT], F32, 4)
        rows = place("rows", [P, 2, GROUP_COLS], F32, 4)
        later = place("later", [P, WINDOW * P], BF16, 2)
        junk = place("junk", [P, PER_UNIT, WINDOW * P], BF16, 2)
        ecol = place("ecol", [P, 3, ETILES], F32, 4)
        ecode = place("ecode", [P, ETILES], F32, 4)
        place_of = place("place_of", [P, ETILES], F32, 4)
        evalue = place("evalue", [P, ETILES], F32, 4)
        epart = place("epart", [P, ETILES], F32, 4)
        eshift = place("eshift", [P, ETILES], F32, 4)
        cnt = place("cnt", [P, PER_UNIT], F32, 4)
        kept = place("kept", [P, PER_UNIT], F32, 4)
        cell = place("cell", [P, ETILES], I32, 4)
        spare = place("spare", [P, ETILES], F32, 4)
        assert at[0] <= nc.sbuf_usable_end, at[0]
        at[0] = keys_end - KT * NODES * 4
        ecol_i = place("ecol_i", [P, 3, ETILES], I32, 4)
        nat_i = place("nat_i", [P, 2, ETILES], I32, 4)
        nat_f = place("nat_f", [P, 2, ETILES], F32, 4)
        ncode = place("ncode", [P, ETILES], F32, 4)
        corner = place("corner", [P, P], F32, 4)
        spare_i = place("spare_i", [P, ETILES], I32, 4)
        assert at[0] <= keys_end, at[0]
        assert at[0] <= nc.sbuf_usable_end, at[0]
        at[0] = shared
        q2 = place("q2", [P, 2, 2, NODES], F32R, 4)
        k2_hi = place("k2_hi", [P, 2, 2, NODES], F32R, 4)
        k2_lo = place("k2_lo", [P, 2, 2, NODES], F32R, 4)
        pt_hi = place("pt_hi", [P, NT, NODES], F32R, 4)
        pt_lo = place("pt_lo", [P, NT, NODES], F32R, 4)
        prob = place("prob", [P, 2, NT, NODES], F32, 4)
        pv_t = place("pv_t", [P, NODES], F32, 4)
        pv_u = place("pv_u", [P, NODES], F32, 4)
        assert at[0] <= nc.sbuf_usable_end, at[0]
        at[0] = shared + NT * FEAT * 4
        ffn_g = place("ffn_g", [P, 2, NODES], F32, 4)
        ffn_h = place("ffn_h", [P, 2, NODES], F32, 4)
        unequal = place("unequal", [P, RING, FEAT], BF16, 2)
        yt = place("yt", [P, 2 * NT, HALF], F32, 4)

        bank = [ctx.enter_context(nc.psum_tensor(f"bank{b}", [P, HALF], F32)) for b in range(8)]

        x_sem = [sem(f"x_sem{s}") for s in range(NT)]
        cols_in = sem("cols_in")
        etw_in = sem("etw_in")
        nat_in = sem("nat_in")
        ecol_in = sem("ecol_in")
        bo_in = sem("bo_in")
        w3s_in = sem("w3s_in")
        codes_out = sem("codes_out")
        rows_in = [sem("rows_in0"), sem("rows_in1")]
        w_in = [sem(f"w_in{r}") for r in range(RING)]
        consts = sem("consts")
        hi_ready = sem("hi_ready")
        lo_ready = sem("lo_ready")
        unit_used = sem("unit_used")
        act_hi = sem("act_hi")
        act_lo = sem("act_lo")
        turned = sem("turned")
        ln_step = [sem(f"ln_step{s}") for s in range(NT)]
        ln_sd = [sem(f"ln_sd{s}") for s in range(NT)]
        normed = sem("normed")
        normed_2 = sem("normed_2")
        first_lo = sem("first_lo")
        spx_ready = sem("spx_ready")
        tok_done = sem("tok_done")
        v2_hi = sem("v2_hi")
        v2_lo = sem("v2_lo")
        resid = sem("resid")
        xbo = sem("xbo")
        code_nat = sem("code_nat")
        e_ready = sem("e_ready")
        w8_ready = sem("w8_ready")
        empty = sem("empty")
        table_in = sem("table_in")
        values = sem("values")
        kept_ready = sem("kept_ready")
        cells = sem("cells")
        scattered = [sem(f"scattered{n}") for n in range(WINDOW)]
        mask_in = sem("mask_in")
        sp_act = sem("sp_act")
        cmp_done = sem("cmp_done")
        k2_in = [sem("k2_in0"), sem("k2_in1")]
        k2_act = sem("k2_act")
        k2_ready = sem("k2_ready")
        q2_act = sem("q2_act")
        q2_ready = sem("q2_ready")
        s_done = sem("s_done")
        masked = sem("masked")
        exped = sem("exped")
        rsum = sem("rsum")
        prob_ready = sem("prob_ready")
        scores_seen = sem("scores_seen")
        pt_done = sem("pt_done")
        pt_h = sem("pt_h")
        pt_l = sem("pt_l")
        pv_done = sem("pv_done")
        pv_half = sem("pv_half")
        pv_sum = sem("pv_sum")
        ot_h = sem("ot_h")
        ot_l = sem("ot_l")
        f_act = sem("f_act")
        f_mul = sem("f_mul")
        f_hi = sem("f_hi")
        f_lo = sem("f_lo")
        y_mul = sem("y_mul")
        y_ready = sem("y_ready")
        out_done = sem("out_done")
        checked = sem("checked")
        summed = sem("summed")
        flag_ready = sem("flag_ready")
        st_done = sem("st_done")
        aggr_done = sem("aggr_done")
        h_done = sem("h_done")

        def f32(ap):
            return ap.bitcast(F32)

        def rows_of(g):
            return codes_flat[GROUP * P * g:min(GROUP * P * g + GROUP_COLS, EDGES)].partition_broadcast(P)

        def ahead(g, uu):
            return RING * g + uu + AHEAD, (uu + AHEAD) % RING, g + 1 + (uu + AHEAD) // RING

        def flag_cell(u):
            b = 6 if u == U_F1 else 4 if u <= U_W3 else 0
            return bank[b][0:1, u - U_F1:u - U_F1 + 1]

        block = ctx.enter_context(nc.Block())

        @block.sync
        def _(sp):
            for s in range(NT):
                sp.dma_start(xs[:, s], x_in[s * P:(s + 1) * P, :]).then_inc(x_sem[s], 16)
            for u in range(RING):
                sp.dma_start(stage[:, u], weights[u]).then_inc(w_in[u], 16)

            def load_group(g, rows_group=None, first=False):
                for uu in range(RING):
                    if first and uu < AHEAD:
                        sp.wait_ge(first_lo, uu + 1)
                    else:
                        sp.wait_ge(lo_ready, RING * g + uu + 1)
                    sp.dma_start(stage[:, uu], weights[RING * g + RING + uu]).then_inc(w_in[uu], 16)
                    if uu == 0 and rows_group is not None:
                        sp.wait_ge(cmp_done, GROUP * (rows_group - 1))
                        load_rows(rows_group)

            sp.dma_start(col[:], cols).then_inc(cols_in, 16)
            sp.dma_start(spx[:, 0], etw.partition_broadcast(P)).then_inc(etw_in, 16)
            sp.dma_start(rowvec[:], bo.partition_broadcast(P)).then_inc(bo_in, 16)
            sp.wait_ge(code_nat, 1)
            sp.dma_start(codes_nat, ncode[:]).then_inc(codes_out, 16)
            sp.wait_ge(codes_out, 16)

            def load_rows(g):
                width = min(GROUP_COLS, EDGES - GROUP * P * g)
                sp.dma_start(rows[:, g % 2, 0:width], rows_of(g)).then_inc(rows_in[g % 2], 16)

            load_rows(0)
            load_rows(1)

            for g in range(8):
                load_group(g, {2: 2, 4: 3, 5: 4, 6: 5}.get(g), first=g == 0)

            def copy_keys(j, jb):
                sp.wait_ge(k2_act, 2 * j + 2)
                sp.dma_start(f32(k2_hi[64:128, jb]), f32(k2_hi[0:64, jb])).then_inc(k2_in[jb], 16)
                sp.wait_ge(k2_ready, j + 1)
                sp.dma_start(f32(k2_lo[64:128, jb]), f32(k2_lo[0:64, jb])).then_inc(k2_in[jb], 16)

            def load(g, uu):
                sp.wait_ge(lo_ready, RING * g + uu + 1)
                sp.dma_start(stage[:, uu], weights[RING * g + RING + uu]).then_inc(w_in[uu], 16)

            load(8, 0)
            load(8, 1)
            load(8, 2)
            load(8, 3)
            copy_keys(0, 0)
            load(9, 0)
            load(9, 1)
            copy_keys(1, 1)
            with sp.Fori(0, 3) as i:
                load(9 + i, 2)
                load(9 + i, 3)
                copy_keys(2 * i + 2, 0)
                load(10 + i, 0)
                load(10 + i, 1)
                copy_keys(2 * i + 3, 1)
            load(12, 2)
            load(12, 3)
            load_group(13)
            for g in range(U_F1 // RING, UNITS // RING - 1):
                for uu in range(RING):
                    sp.wait_ge(checked, RING * g + uu - U_F1 + 1)
                    load(g, uu)
            sp.wait_ge(xbo, NT)
            sp.dma_start(rowvec[:], w3_s.partition_broadcast(P)).then_inc(w3s_in, 16)
            for n in range(2 * NT):
                h, s = n // NT, n % NT
                sp.wait_ge(y_ready, n + 1)
                sp.dma_start(out[s * P:(s + 1) * P, h * HALF:(h + 1) * HALF], yt[:, n]).then_inc(out_done, 16)
            sp.wait_ge(out_done, 16 * 2 * NT)

        @block.gpsimd
        def _(pool):
            pool.sem_inc(ot_l, 1)
            pool.memset(ident[:], 0.0).then_inc(consts, 1)
            pool.wait_ge(consts, 1)
            pool.affine_select(out=ident[:], in_=ident[:], compare_op=ALU.not_equal, fill=1.0, base=0,
                               pattern=[[-1, P]], channel_multiplier=1).then_inc(consts, 1)
            pool.memset(ones[:], 1.0).then_inc(consts, 1)
            pool.memset(later[:], 1.0).then_inc(consts, 1)
            pool.memset(mask8[:], -ABSENT).then_inc(consts, 1)
            pool.iota(spare_i[:], pattern=[[0, ETILES // WINDOW], [P, WINDOW]], base=CELLS,
                      channel_multiplier=1).then_inc(consts, 1)
            pool.wait_ge(consts, 6)
            pool.affine_select(out=later[:], in_=later[:], compare_op=ALU.is_gt, fill=0.0, base=0,
                               pattern=[[1, WINDOW * P]], channel_multiplier=-1).then_inc(consts, 1)
            for u in range(AHEAD):
                pool.wait_ge(hi_ready, u + 1)
                pool.tensor_tensor(w_lo[:, u], stage[:, u], f32(w_hi[:, u]), ALU.subtract).then_inc(first_lo, 1)
            pool.wait_ge(e_ready, 7)
            pool.wait_ge(w8_ready, 2)
            pool.tensor_scalar(evalue[:], place_of[:], 0.0, w8[:, 0:1], ALU.is_equal, ALU.mult).then_inc(values, 1)
            for n in range(1, 4):
                pool.tensor_scalar(epart[:], place_of[:], float(n), w8[:, n:n + 1], ALU.is_equal, ALU.mult).then_inc(values, 1)
                pool.wait_ge(values, 2 * n)
                pool.tensor_tensor(evalue[:], evalue[:], epart[:], ALU.add).then_inc(values, 1)
                pool.wait_ge(values, 2 * n + 1)
            pool.wait_ge(empty, NT)
            pool.dma_start(table_nat, mask8[:]).then_inc(table_in, 16)
            pool.wait_ge(table_in, 16)
            for t in range(ETILES):
                pool.wait_ge(cells, t + 1)
                if t >= WINDOW:
                    pool.wait_ge(scattered[t % WINDOW], 16 * (t // WINDOW))
                pool.indirect_dma_start(out=table, out_offset=bass.IndirectOffsetOnAxis(ap=cell[:, t:t + 1], axis=0),
                                        in_=evalue[:, t:t + 1], in_offset=None).then_inc(scattered[t % WINDOW], 16)
            for landed in scattered:
                pool.wait_ge(landed, 16 * (ETILES // WINDOW))
            pool.dma_start(mask8[:], table_nat).then_inc(mask_in, 16)
            pool.wait_ge(bo_in, 16)
            for s in range(NT):
                pool.wait_ge(normed, 2 * s + 2) if s < 2 else pool.wait_ge(normed_2, 2)
                pool.tensor_tensor(xs[:, s], xs[:, s], rowvec[:], ALU.add).then_inc(xbo, 1)

            def split_ahead(g, uu):
                v, slot, _ = ahead(g, uu)
                pool.wait_ge(hi_ready, v + 1)
                pool.tensor_tensor(w_lo[:, slot], stage[:, slot], f32(w_hi[:, slot]), ALU.subtract).then_inc(lo_ready, 1)

            def attention(i, last):
                for jj in range(2):
                    if not (last and jj == 1):
                        split_ahead(8 + i + jj, (3 + 2 * jj) % RING)
                        split_ahead(9 + i, 2 * jj)
                    pool.wait_ge(ot_h, 2 * i + jj + 1)
                    pool.tensor_tensor(xt_lo[:, 2 * i + jj], pv_u[:], f32(xt_hi[:, 2 * i + jj]),
                                       ALU.subtract).then_inc(ot_l, 1)

            pool.wait_ge(lo_ready, ahead(8, 3)[0])
            with pool.Fori(0, 3) as i:
                attention(i, False)
            attention(3, True)
            pool.wait_ge(lo_ready, U_F1)
            for u in range(U_F1, UNITS):
                split_ahead(u // RING, u % RING - AHEAD)

        @block.scalar
        def _(act):
            act.dma_start(ecol_i[:], edge_cols).then_inc(ecol_in, 16)
            act.dma_start(nat_i[:], src_dst.rearrange("t p f -> p t f")).then_inc(nat_in, 16)

            def split_hi(v, slot, count):
                act.wait_ge(w_in[slot], 16 * count)
                nc.scalar.activation(w_hi[:, slot], stage[:, slot], ACT.Copy).then_inc(hi_ready, 1)

            def split_ahead(g, uu):
                v, slot, count = ahead(g, uu)
                act.wait_ge(unit_used, v - (RING - 1) + 1)
                split_hi(v, slot, count)

            def layernorm(n):
                def deviation(s):
                    act.wait_ge(ln_step[s], LN_STEPS[s] * n + 1)
                    nc.scalar.activation(sd[:, s:s + 1], ve[:, s:s + 1], ACT.Sqrt).then_inc(ln_sd[s], 1)

                deviation(0)
                for s in range(2):
                    if n == 0 and s == 1:
                        split_hi(0, 0, 1)
                        deviation(2)
                    act.wait_ge(ln_step[s], LN_STEPS[s] * n + LN_STEPS[s])
                    for hf in (slice(0, HALF), slice(HALF, FEAT)):
                        nc.scalar.activation(xn[:, s, hf], xs[:, s, hf], ACT.Identity, scale=rstd[:, s:s + 1],
                                             bias=shift[:, s:s + 1]).then_inc(normed, 1)
                    if n == 1 or s == 0:
                        deviation(s + 1)

            def turned_hi(n):
                for f in range(KT):
                    act.wait_ge(turned, KT * n + f + 1)
                    nc.scalar.activation(xt_hi[:, f], bank[TURN_BANKS[f]][:, 0:NODES], ACT.Copy).then_inc(act_hi, 1)

            layernorm(0)
            turned_hi(0)
            split_hi(1, 1, 1)
            split_hi(2, 2, 1)
            act.wait_ge(cols_in, 16)

            def project(g, uu, tile, bias):
                act.wait_ge(unit_used, RING * g + uu + 1 + 1)
                nc.scalar.activation(qk_hi[:, tile], bank[uu][:, 0:NODES], ACT.Identity,
                                     bias=col[:, bass.ds(bias, 1)]).then_inc(act_hi, 1)

            for n in range(KT):
                project(n // RING, n % RING, n, C_BV + n)
                if n == 0:
                    act.wait_ge(spx_ready, 2)
                    nc.scalar.activation(spx[:, 2], spx[:, 1], ACT.Exp).then_inc(sp_act, 1)
                    act.wait_ge(sp_act, 1)
                    nc.scalar.activation(spx[:, 3], spx[:, 2], ACT.Ln, bias=1.0).then_inc(sp_act, 1)
                split_ahead(n // RING, n % RING)
                if n == 1:
                    act.wait_ge(sp_act, 2)
                    nc.scalar.activation(spx[:, 2], spx[:, 1], ACT.Exp)
            for i in range(2):
                for uu in range(RING):
                    split_ahead(i + 2, uu)
                for s in range(NT):
                    if s < NT - 1:
                        act.wait_ge(tok_done, 2 * i + s + 1)
                    else:
                        act.wait_ge(unit_used, U_IV + RING * i + RING + 1)
                    nc.scalar.activation(v2[:, s, 8 * i:8 * i + 8, 0:HD],
                                         bank[V2_BANKS[i][s]][:].rearrange("p (h d) -> p h d", d=HD),
                                         ACT.Copy).then_inc(v2_hi, 1)
            with act.Fori(0, 4) as i:
                for uu in range(RING):
                    split_ahead(i + 4, uu)
                    project(i + 4, uu, RING * i + uu, C_BQ + RING * i + uu)

            def keys_hi(j, jb):
                act.wait_ge(unit_used, U_AT + 2 * j + 1 + 1)
                for hh in range(2):
                    r = slice(64 * hh, 64 * hh + 64)
                    nc.scalar.activation(k2_hi[0:64, jb, hh], bank[0][r, 0:NODES], ACT.Identity,
                                         bias=col[r, bass.ds(C_BIK + 2 * j + hh, 1)]).then_inc(k2_act, 1)

            def queries_hi(j, jb):
                act.wait_ge(unit_used, U_AT + 2 * j + 2 + 1)
                for hh in range(2):
                    r = slice(64 * hh, 64 * hh + 64)
                    nc.scalar.activation(q2[0:64, jb, hh], bank[1][r, 0:NODES], ACT.Identity,
                                         bias=col[r, bass.ds(C_BIQ + 2 * j + hh, 1)]).then_inc(q2_act, 1)

            def exps(h, hh):
                for s in range(NT):
                    act.wait_ge(masked, 3 * h + s + 1)
                    nc.scalar.activation(prob[:, hh, s], prob[:, hh, s], ACT.Exp, scale=-1.0,
                                         bias=negmax[:, hh, s:s + 1], accum_out=psums[:, hh, s:s + 1]).then_inc(exped, 1)

            def probs_t(h, hh):
                for m in range(NT):
                    act.wait_ge(pt_done, 3 * h + m + 1)
                    nc.scalar.activation(pt_hi[:, m], bank[PROB_BANKS[hh][m]][:, 0:NODES], ACT.Copy).then_inc(pt_h, 1)

            def head_half(h):
                act.wait_ge(pv_done, h + 1)
                act.wait_ge(pv_sum, h + 1)
                nc.scalar.activation(pv_t[0:64, :], bank[7][64:128, 0:NODES], ACT.Identity,
                                     bias=col[64:128, bass.ds(C_BIV + h, 1)]).then_inc(pv_half, 1)

            def pair_hi(j):
                act.wait_ge(pv_sum, 2 * j + 2 + 1)
                nc.scalar.activation(xt_hi[:, j], pv_u[:], ACT.Copy).then_inc(ot_h, 1)

            split_ahead(8, 0)
            keys_hi(0, 0)
            split_ahead(8, 1)
            queries_hi(0, 0)
            split_ahead(8, 2)
            keys_hi(1, 1)

            def attention(i, last):
                for jj in range(2):
                    a = 4 * i + 2 * jj
                    more = not (last and jj == 1)
                    exps(a + 1, 1)
                    if more:
                        queries_hi(2 * i + jj + 1, (jj + 1) % 2)
                        split_ahead(8 + i + jj, (3 + 2 * jj) % RING)
                    probs_t(a, 0)
                    head_half(a)
                    probs_t(a + 1, 1)
                    if not last:
                        keys_hi(2 * i + jj + 2, jj)
                    if more:
                        split_ahead(9 + i, 2 * jj)
                    head_half(a + 1)
                    if more:
                        exps(a + 2, 0)
                    pair_hi(2 * i + jj)

            exps(0, 0)
            with act.Fori(0, 3) as i:
                attention(i, False)
            attention(3, True)
            for n in range(1, 7):
                split_ahead(12 + n // RING, n % RING)
            layernorm(1)
            turned_hi(1)
            split_ahead(13, 3)

            def hidden_hi(n, tile):
                act.wait_ge(f_mul, n + 1) if n < 4 else act.wait_ge(f_act, n + 1)
                src = ffn_h if n < 4 else ffn_g
                nc.scalar.activation(qk_hi[:, tile], src[:, n % 2], ACT.Copy).then_inc(f_hi, 1)

            for j in range(4):
                split_ahead(14 + j // 2, 2 * (j % 2))
                act.wait_ge(unit_used, U_F1 + 2 * j + 1 + 1)
                if j >= 2:
                    act.wait_ge(f_mul, j - 1)
                nc.scalar.activation(ffn_g[:, j % 2], bank[2 * (j % 2)][:, 0:NODES], ACT.Silu,
                                     scale=col[:, C_S1 + j:C_S1 + j + 1]).then_inc(f_act, 1)
                split_ahead(14 + j // 2, 2 * (j % 2) + 1)
                hidden_hi(j, j)
            for n in range(4, 12):
                layer, o = (n - 4) // 4, n % 4
                if n % 2 == 0 and n // 2 - 2 + U_H1 + AHEAD < UNITS:
                    split_ahead(16, n // 2 - 2)
                if n % 2:
                    act.wait_ge(unit_used, U_H1 + (n - 4) // 2 + 1 + 1)
                else:
                    act.wait_ge(h_done, n // 2 - 1)
                act.wait_ge(f_lo, n - 1)
                nc.scalar.activation(ffn_g[:, n % 2], bank[n % 4][:, 0:NODES], ACT.Gelu,
                                     scale=col[:, C_H1 + n - 4:C_H1 + n - 3]).then_inc(f_act, 1)
                hidden_hi(n, n)
            split_ahead(17, 0)

        @block.vector
        def _(dve):
            dve.sem_inc(pv_sum, 1)
            dve.sem_inc(lo_ready, AHEAD)

            def split_lo(v, slot):
                dve.wait_ge(hi_ready, v + 1)
                nc.vector.tensor_tensor(w_lo[:, slot], stage[:, slot], f32(w_hi[:, slot]),
                                        ALU.subtract).then_inc(lo_ready, 1)

            def split_ahead(g, uu):
                v, slot, _ = ahead(g, uu)
                split_lo(v, slot)

            def batch_stats(s, halves, last_of_tile=True):
                for hf in halves:
                    last = nc.vector.bn_stats(stats[:, s, hf], xs[:, s, hf * HALF:(hf + 1) * HALF])
                if last_of_tile:
                    last.then_inc(st_done, 1)

            def moments(n, s):
                dve.wait_ge(st_done, NT * n + s + 1)
                nc.vector.bn_aggr(mv[:, s], stats[:, s].rearrange("p a b -> p (a b)")).then_inc(aggr_done, 1)

            def variance(n, s):
                dve.wait_ge(aggr_done, NT * n + s + 1)
                nc.vector.tensor_scalar(ve[:, s:s + 1], mv[:, s, 1:2], EPS, None, ALU.add).then_inc(ln_step[s], 1)

            def inverse(n, s, steps):
                r, t = rstd[:, s:s + 1], tmp3[:, s:s + 1]
                for k in steps:
                    if k == 0:
                        dve.wait_ge(ln_sd[s], n + 1)
                        ins = nc.vector.reciprocal(r, sd[:, s:s + 1])
                    else:
                        dve.wait_ge(ln_step[s], LN_STEPS[s] * n + k + 1)
                        if k == 1:
                            ins = nc.vector.scalar_tensor_tensor(out=t, in0=r, scalar=-0.5, in1=r, op0=ALU.mult, op1=ALU.mult)
                        elif k == 2:
                            ins = nc.vector.tensor_tensor(t, t, ve[:, s:s + 1], ALU.mult)
                        elif k == 3:
                            ins = nc.vector.scalar_tensor_tensor(out=r, in0=t, scalar=1.5, in1=r, op0=ALU.add, op1=ALU.mult)
                        else:
                            ins = nc.vector.scalar_tensor_tensor(out=shift[:, s:s + 1], in0=mv[:, s, 0:1], scalar=-1.0,
                                                                 in1=r, op0=ALU.mult, op1=ALU.mult)
                    ins.then_inc(ln_step[s], 1)

            def normalise_nodes(n, s):
                dve.wait_ge(ln_step[s], LN_STEPS[s] * (n + 1))
                for hf in (slice(0, HALF), slice(HALF, FEAT)):
                    nc.vector.tensor_scalar(xn[:, s, hf], xs[:, s, hf], mv[:, s, 0:1], rstd[:, s:s + 1],
                                            ALU.subtract, ALU.mult).then_inc(normed_2, 1)

            def turned_lo(n):
                for f in range(KT):
                    dve.wait_ge(act_hi, 4 * KT * n + f + 1)
                    nc.vector.tensor_tensor(xt_lo[:, f], bank[TURN_BANKS[f]][:, 0:NODES], f32(xt_hi[:, f]),
                                            ALU.subtract).then_inc(act_lo, 1)

            dve.wait_ge(x_sem[0], 16)
            batch_stats(0, (0, 1))
            moments(0, 0)
            variance(0, 0)
            inverse(0, 0, range(5))
            dve.wait_ge(x_sem[1], 16)
            batch_stats(1, (0, 1))
            dve.wait_ge(nat_in, 16)
            nc.vector.tensor_copy(nat_f[:], nat_i[:]).then_inc(e_ready, 1)
            moments(0, 1)
            dve.wait_ge(e_ready, 1)
            nc.vector.scalar_tensor_tensor(out=ncode[:], in0=nat_f[:, 0], scalar=float(NODES), in1=nat_f[:, 1],
                                           op0=ALU.mult, op1=ALU.add).then_inc(code_nat, 1)
            variance(0, 1)
            dve.wait_ge(x_sem[2], 16)
            batch_stats(2, (0,), False)
            inverse(0, 1, (0,))
            batch_stats(2, (1,))
            inverse(0, 1, (1,))
            moments(0, 2)
            inverse(0, 1, (2,))
            variance(0, 2)
            inverse(0, 1, (3, 4))
            inverse(0, 2, range(4))
            normalise_nodes(0, 2)
            dve.wait_ge(ecol_in, 16)
            nc.vector.tensor_copy(ecol[:], ecol_i[:]).then_inc(e_ready, 1)
            dve.wait_ge(consts, 7)
            nc.vector.tensor_copy(spare[:], spare_i[:]).then_inc(e_ready, 1)
            dve.wait_ge(e_ready, 2)
            nc.vector.tensor_scalar(place_of[:], ecol[:, 2], 0.0, 4.0, ALU.is_equal, ALU.mult).then_inc(e_ready, 1)
            nc.vector.scalar_tensor_tensor(out=ecode[:], in0=ecol[:, 0], scalar=float(NODES), in1=ecol[:, 1],
                                           op0=ALU.mult, op1=ALU.add).then_inc(e_ready, 1)
            dve.wait_ge(e_ready, 5)
            nc.vector.scalar_tensor_tensor(out=place_of[:], in0=ecol[:, 2], scalar=-1.0, in1=place_of[:],
                                           op0=ALU.add, op1=ALU.add).then_inc(e_ready, 1)
            nc.vector.tensor_tensor(eshift[:], ecode[:], spare[:], ALU.subtract).then_inc(e_ready, 1)
            turned_lo(0)
            dve.wait_ge(etw_in, 16)
            nc.vector.tensor_scalar(spx[:, 1], spx[:, 0], -1.0, None, ALU.mult).then_inc(spx_ready, 1)
            dve.wait_ge(spx_ready, 1)
            nc.vector.tensor_tensor(spx[:, 1], spx[:, 1], spx[:, 0], ALU.min).then_inc(spx_ready, 1)

            def compare(u):
                for d in range(PER_UNIT):
                    t = PER_UNIT * u + d
                    g, lo = t // GROUP, P * (t % GROUP)
                    if t % GROUP == 0:
                        dve.wait_ge(rows_in[g % 2], 16 * (g // 2 + 1))
                    w = min(WINDOW, ETILES - t) * P
                    nc.vector.scalar_tensor_tensor(
                        out=junk[:, d, 0:w], in0=rows[:, g % 2, lo:lo + w], scalar=ecode[:, t:t + 1],
                        in1=later[:, 0:w], op0=ALU.is_equal, op1=ALU.mult, accum_out=cnt[:, d:d + 1]).then_inc(cmp_done, 1)

            def keep(u):
                dve.wait_ge(cmp_done, PER_UNIT * (u + 1))
                nc.vector.scalar_tensor_tensor(out=kept[:], in0=cnt[:], scalar=0.0, in1=eshift[:, PER_UNIT * u:PER_UNIT * (u + 1)],
                                               op0=ALU.is_equal, op1=ALU.mult).then_inc(kept_ready, 1)

            def locate(u):
                dve.wait_ge(kept_ready, u + 1)
                tiles = slice(PER_UNIT * u, PER_UNIT * (u + 1))
                nc.vector.tensor_tensor(cell[:, tiles], kept[:], spare[:, tiles], ALU.add).then_inc(cells, PER_UNIT)

            def project_lo(n, uu, tile, bias):
                dve.wait_ge(act_hi, KT + n + 1)
                nc.vector.scalar_tensor_tensor(
                    out=qk_lo[:, tile], in0=bank[uu][:, 0:NODES], scalar=col[:, bass.ds(bias, 1)],
                    in1=f32(qk_hi[:, tile]), op0=ALU.add, op1=ALU.subtract).then_inc(act_lo, 1)

            dve.wait_ge(cols_in, 16)
            project_lo(0, 0, 0, C_BV)
            dve.wait_ge(e_ready, 7)
            compare(0)
            keep(0)
            dve.wait_ge(sp_act, 2)
            nc.vector.scalar_tensor_tensor(out=w8[:], in0=spx[:, 0], scalar=0.0, in1=spx[:, 3],
                                           op0=ALU.max, op1=ALU.add).then_inc(w8_ready, 1)
            dve.wait_ge(w8_ready, 1)
            nc.vector.tensor_scalar(w8[:], w8[:], 8.0, None, ALU.mult).then_inc(w8_ready, 1)
            nc.vector.tensor_scalar(corner[:], ident[:], 1.0, ABSENT, ALU.subtract, ALU.mult).then_inc(w8_ready, 1)
            dve.wait_ge(w8_ready, 3)
            for s in range(NT):
                nc.vector.scalar_tensor_tensor(out=mask8[:, s, s * P:(s + 1) * P], in0=ident[:], scalar=w8[:, 3:4],
                                               in1=corner[:], op0=ALU.mult, op1=ALU.add).then_inc(empty, 1)
            locate(0)
            split_ahead(0, 0)
            for n in range(1, KT):
                project_lo(n, n % RING, n, C_BV + n)
                compare(n)
                split_ahead(n // RING, n % RING)
                keep(n)
                locate(n)

            def v2_parts(hf):
                for s in range(NT):
                    dve.wait_ge(v2_hi, NT * hf + s + 1)
                    heads = slice(8 * hf, 8 * hf + 8)
                    nc.vector.tensor_tensor(v2[:, s, heads, HD:2 * HD], bank[V2_BANKS[hf][s]][:].rearrange("p (h d) -> p h d", d=HD),
                                            f32(v2[:, s, heads, 0:HD]), ALU.subtract).then_inc(v2_lo, 1)

            for n in range(KT):
                compare(KT + n)
                split_ahead(2 + n // RING, n % RING)
                keep(KT + n)
                if n % RING == RING - 1:
                    v2_parts(n // RING)
                locate(KT + n)
            for n in range(2 * KT):
                compare(2 * KT + n)
                split_ahead(4 + n // RING, n % RING)
                keep(2 * KT + n)
                project_lo(KT + n, n % RING, n, C_BQ + n)
                locate(2 * KT + n)

            def keys_lo(j, jb):
                for hh in range(2):
                    dve.wait_ge(k2_act, 2 * j + hh + 1)
                    last = nc.vector.scalar_tensor_tensor(
                        out=k2_lo[0:64, jb, hh], in0=bank[0][64 * hh:64 * hh + 64, 0:NODES],
                        scalar=col[0:64, bass.ds(C_BIK + 2 * j + hh, 1)], in1=f32(k2_hi[0:64, jb, hh]),
                        op0=ALU.add, op1=ALU.subtract)
                last.then_inc(k2_ready, 1)

            def queries_lo(j, jb):
                for hh in range(2):
                    dve.wait_ge(q2_act, 2 * j + hh + 1)
                    r = slice(64 * hh, 64 * hh + 64)
                    last = nc.vector.scalar_tensor_tensor(
                        out=q2[64:128, jb, hh], in0=bank[1][r, 0:NODES],
                        scalar=col[0:64, bass.ds(C_BIQ + 2 * j + hh, 1)], in1=f32(q2[0:64, jb, hh]),
                        op0=ALU.add, op1=ALU.subtract)
                last.then_inc(q2_ready, 1)

            def mask_scores(h, hh, s):
                dve.wait_ge(s_done, 3 * h + s + 1)
                dve.sem_inc(scores_seen, 1)
                nc.vector.tensor_tensor_reduce(prob[:, hh, s], bank[2 + s][:, 0:NODES], mask8[:, s], -SCALE, 3e38,
                                               ALU.add, ALU.min, negmax[:, hh, s:s + 1]).then_inc(masked, 1)

            def normalise(h, hh, tiles):
                for s in range(tiles[0], tiles[-1] + 2):
                    if s in tiles:
                        dve.wait_ge(exped, 3 * h + s + 1)
                        nc.vector.reciprocal(rsums[:, hh, s:s + 1], psums[:, hh, s:s + 1]).then_inc(rsum, 1)
                    if s > tiles[0]:
                        dve.wait_ge(rsum, 3 * h + s)
                        nc.vector.tensor_scalar(prob[:, hh, s - 1], prob[:, hh, s - 1], rsums[:, hh, s - 1:s], None,
                                                ALU.mult).then_inc(prob_ready, 1)

            def probs_lo(h, hh, m):
                dve.wait_ge(pt_h, 3 * h + m + 1)
                nc.vector.tensor_tensor(pt_lo[:, m], bank[PROB_BANKS[hh][m]][:, 0:NODES], f32(pt_hi[:, m]),
                                        ALU.subtract).then_inc(pt_l, 1)

            def head_sum(h, hh, j):
                r = slice(64 * hh, 64 * hh + 64)
                dve.wait_ge(pv_half, h + 1)
                dve.wait_ge(ot_l, j + 1)
                nc.vector.tensor_tensor(pv_u[r, :], bank[7][0:64, 0:NODES], pv_t[0:64, :], ALU.add).then_inc(pv_sum, 1)

            split_ahead(8, 0)
            keys_lo(0, 0)
            split_ahead(8, 1)
            queries_lo(0, 0)
            split_ahead(8, 2)
            keys_lo(1, 1)

            def attention(i, last):
                for jj in range(2):
                    j = 2 * i + jj
                    a, b = 4 * i + 2 * jj, 4 * i + 2 * jj + 1
                    normalise(a, 0, (0, 1))
                    mask_scores(b, 1, 0)
                    normalise(a, 0, (2,))
                    mask_scores(b, 1, 1)
                    mask_scores(b, 1, 2)
                    normalise(b, 1, (0, 1, 2))
                    if not (last and jj == 1):
                        queries_lo(j + 1, (jj + 1) % 2)
                    for m in range(NT):
                        probs_lo(a, 0, m)
                    probs_lo(b, 1, 0)
                    head_sum(a, 0, j)
                    probs_lo(b, 1, 1)
                    probs_lo(b, 1, 2)
                    if not (last and jj == 1):
                        for s in range(NT):
                            mask_scores(b + 1, 0, s)
                    if not last:
                        keys_lo(j + 2, jj)
                    head_sum(b, 1, j)

            dve.wait_ge(mask_in, 16)
            for s in range(NT):
                mask_scores(0, 0, s)
            with dve.Fori(0, 3) as i:
                attention(i, False)
            attention(3, True)
            dve.wait_ge(lo_ready, ahead(12, 1)[0])

            def residual(h, s):
                if s < NT - 1:
                    dve.wait_ge(tok_done, 4 + 2 * h + s + 1)
                else:
                    dve.wait_ge(unit_used, U_WO + RING * h + RING + 1)
                xh = xs[:, s, h * HALF:(h + 1) * HALF]
                nc.vector.tensor_tensor(xh, bank[3 * h + s][:], xh, ALU.add).then_inc(resid, 1)

            for uu in range(1, RING):
                split_ahead(12, uu)
            dve.wait_ge(xbo, NT)
            for s in range(NT):
                residual(0, s)
            dve.wait_ge(resid, NT)
            for s in range(NT):
                batch_stats(s, (0,), False)
            def check(u):
                n = u - U_F1
                dve.wait_ge(hi_ready, u + 1)
                if n >= RING:
                    dve.wait_ge(checked, n - RING + 1)
                nc.vector.scalar_tensor_tensor(
                    out=unequal[:, u % RING], in0=stage[:, u % RING], scalar=0.0, in1=f32(w_hi[:, u % RING]),
                    op0=ALU.add, op1=ALU.not_equal, accum_out=inexact[:, n:n + 1]).then_inc(checked, 1)

            def flag(u):
                n = u - U_F1
                dve.wait_ge(summed, FFN_UNITS if u >= UNITS - 2 else n + 1)
                nc.vector.tensor_copy(flags[0:1, n:n + 1], flag_cell(u)).then_inc(flag_ready, 1)

            split_ahead(13, 0)
            check(U_F1)
            check(U_F1 + 1)
            for s in range(NT):
                residual(1, s)
                dve.wait_ge(resid, NT + s + 1)
                batch_stats(s, (1,))
                moments(1, s)
                variance(1, s)
                inverse(1, s, range(LN_STEPS[s] - 1))
                if s == 0:
                    flag(U_F1)
            normalise_nodes(1, 2)
            turned_lo(1)
            check(U_F1 + 2)

            def hidden_lo(n):
                src = ffn_h if n < 4 else ffn_g
                dve.wait_ge(f_hi, n + 1)
                nc.vector.tensor_tensor(qk_lo[:, n], src[:, n % 2], f32(qk_hi[:, n]), ALU.subtract).then_inc(f_lo, 1)

            for j in range(4):
                for u in (U_F1 + 2 * j, U_F1 + 2 * j + 1):
                    check(u + AHEAD)
                    flag(u + 1)
                dve.wait_ge(f_act, j + 1)
                dve.wait_ge(unit_used, U_F1 + 2 * j + 2 + 1)
                nc.vector.scalar_tensor_tensor(out=ffn_h[:, j % 2], in0=bank[2 * (j % 2) + 1][:, 0:NODES],
                                               scalar=col[:, C_S2 + j:C_S2 + j + 1], in1=ffn_g[:, j % 2],
                                               op0=ALU.mult, op1=ALU.mult).then_inc(f_mul, 1)
                hidden_lo(j)
            for n in range(4, 12):
                if n % 2 == 0:
                    check(U_H1 + n // 2 - 2 + AHEAD)
                    flag(U_H1 + n // 2 - 2 + 1)
                hidden_lo(n)
            check(UNITS - 1)
            for u in range(U_W3 + 1, UNITS):
                flag(u)
            dve.wait_ge(w3s_in, 16)
            for n in range(2 * NT):
                h, s = n // NT, n % NT
                if s < NT - 1:
                    dve.wait_ge(tok_done, 8 + 2 * h + s + 1)
                else:
                    dve.wait_ge(unit_used, U_W3 + 2 * h + 2 + 1)
                nc.vector.tensor_tensor(yt[:, n], bank[5 - 3 * h + s][:], rowvec[:, h * HALF:(h + 1) * HALF],
                                        ALU.mult).then_inc(y_mul, 1)
                dve.wait_ge(y_mul, n + 1)
                nc.vector.tensor_tensor(yt[:, n], yt[:, n], xs[:, s, h * HALF:(h + 1) * HALF], ALU.add).then_inc(y_ready, 1)

        @block.tensor
        def _(pe):
            pe.sem_inc(unit_used, 1)

            def warm_up(count):
                for _ in range(count):
                    nc.tensor.transpose(bank[TURN_BANKS[-1]][:, 0:P], ident[:], ident[:])

            def turn(n):
                for s in range(NT):
                    for f in range(KT):
                        if f % 4 == 0:
                            half = f // 4 + 1
                            pe.wait_ge(normed, 4 * n + 2 * s + half) if s < 2 else pe.wait_ge(normed_2, 2 * n + half)
                        if n == 1 and s == 0 and f == 3:
                            pe.wait_ge(flag_ready, 1)
                        if n == 1 and s == 0 and f >= 5:
                            pe.wait_ge(resid, NT + f - 4)
                        last = nc.tensor.transpose(bank[TURN_BANKS[f]][:, s * P:(s + 1) * P], xn[:, s, f * P:(f + 1) * P], ident[:])
                        if s == NT - 1:
                            last.then_inc(turned, 1)

            def by_weight(slot, offset, kt, acts, a0, dst, passes, ready=None):
                n, last_n = 0, 3 * kt - 1
                for k in range(kt):
                    if ready is not None and passes[0] <= n < passes[1]:
                        pe.wait_ge(ready[0], ready[1] + k)
                    w = slice(offset + k * P, offset + (k + 1) * P)
                    for wp, ap in ((w_hi, acts[0]), (w_hi, acts[1]), (w_lo, acts[0])):
                        if passes[0] <= n < passes[1]:
                            last = nc.tensor.matmul(dst[:, 0:NODES], wp[:, slot, w], ap[:, a0 + k], start=n == 0, stop=n == last_n)
                        n += 1
                return last

            ALLP = (0, 24)
            XT, QK = (xt_hi, xt_lo), (qk_hi, qk_lo)

            def node_tile(slot, pair, pairs, acts, a0, dst, s, parts=(0, 1)):
                for k2 in parts:
                    k = 2 * pair + k2
                    a = slice(s * P, (s + 1) * P)
                    c = slice(k2 * HALF, (k2 + 1) * HALF)
                    for m, (ap, wp) in enumerate(((acts[0], w_hi), (acts[0], w_lo), (acts[1], w_hi))):
                        last = nc.tensor.matmul(dst[:], ap[:, a0 + k, a], wp[:, slot, c],
                                                start=k == 0 and m == 0, stop=k == 2 * pairs - 1 and m == 2)
                return last

            def by_nodes(slot, pair, pairs, acts, a0, banks):
                for s in range(NT):
                    last = node_tile(slot, pair, pairs, acts, a0, banks[s], s)
                    if pair == pairs - 1 and s < NT - 1:
                        last.then_inc(tok_done, 1)
                last.then_inc(unit_used, 1)

            pe.wait_ge(consts, 2)
            warm_up(WARM_UP)
            turn(0)
            pe.wait_ge(hi_ready, 1)
            for k in range(KT):
                pe.wait_ge(act_lo, k + 1)
                for m in range(2):
                    nc.tensor.matmul(bank[0][:, 0:NODES], w_hi[:, 0, k * P:(k + 1) * P], (xt_hi, xt_lo)[m][:, k],
                                     start=k == 0 and m == 0, stop=False)
            pe.wait_ge(first_lo, 1)
            for k in range(KT):
                last = nc.tensor.matmul(bank[0][:, 0:NODES], w_lo[:, 0, k * P:(k + 1) * P], xt_hi[:, k],
                                        start=False, stop=k == KT - 1)
            last.then_inc(unit_used, 1)
            def project(n, tile):
                if n < AHEAD:
                    pe.wait_ge(first_lo, n + 1)
                else:
                    pe.wait_ge(lo_ready, n + 1)
                if tile >= RING:
                    pe.wait_ge(act_lo, KT + tile - RING + 1)
                if tile in (KT + 2, KT + 3):
                    pe.wait_ge(v2_lo, NT + tile - KT)
                by_weight(n % RING, 0, KT, XT, 0, bank[n % RING], ALLP).then_inc(unit_used, 1)

            for n in range(1, KT):
                project(n, n)
            for n in range(KT):
                pe.wait_ge(lo_ready, U_IV + n + 1)
                pe.wait_ge(act_lo, KT + 2 * (n % RING) + 2)
                by_nodes(n % RING, n % RING, RING, QK, 0, [bank[b] for b in V2_BANKS[n // RING]])
            for n in range(KT, 3 * KT):
                project(KT + n, n)

            def inner(u, b, parts, ready, j, tiles=None):
                if parts[0] == 0:
                    pe.wait_ge(lo_ready, u + 1)
                    pe.wait_ge(ready, j)
                last = by_weight(u % RING, 0, KT, QK, KT * (1 - b), bank[b], parts, tiles)
                if parts[1] == 24:
                    last.then_inc(unit_used, 1)

            def scores(h, s):
                j = h // 2
                if s == 0:
                    pe.wait_ge(k2_in[j % 2], 32 * (j // 2 + 1))
                    pe.wait_ge(q2_ready, j + 1)
                if h:
                    pe.wait_ge(masked, 3 * h + s - 2)
                if h and h % 2 == 0 and s != 1:
                    pe.wait_ge(pt_l, 3 * h - 3 + s // 2)
                for n, k2 in enumerate((k2_hi, k2_lo)):
                    last = nc.tensor.matmul(bank[2 + s][:, 0:NODES], q2[:, j % 2, h % 2, s * P:(s + 1) * P], k2[:, j % 2, h % 2],
                                            start=n == 0, stop=n == 1)
                last.then_inc(s_done, 1)

            def turn_probs(h, m):
                if m == 0:
                    pe.wait_ge(prob_ready, 3 * h + 3)
                b = PROB_BANKS[h % 2][m]
                if b < 5:
                    pe.wait_ge(masked, 3 * (h | 1) + b - 1)
                elif h:
                    pe.wait_ge(pt_l, 3 * h + (m - 1 if h % 2 == 0 else m - 3))
                for s in range(NT):
                    last = nc.tensor.transpose(bank[b][:, s * P:(s + 1) * P],
                                               prob[:, h % 2, s, m * P:(m + 1) * P], ident[:])
                last.then_inc(pt_done, 1)

            def weigh(h):
                pe.wait_ge(pv_sum, h + 1)
                for m in range(NT):
                    pe.wait_ge(pt_l, 3 * h + m + 1)
                    for n, pt in enumerate((pt_hi, pt_lo)):
                        last = nc.tensor.matmul(bank[7][:, 0:NODES], v2[:, m, h], pt[:, m],
                                                start=m == 0 and n == 0, stop=m == NT - 1 and n == 1)
                last.then_inc(pv_done, 1)

            pairs = HEADS // 2
            pe.wait_ge(act_lo, 3 * KT + RING + 1)
            inner(U_AT, 0, (0, 24), k2_ready, 0, (act_lo, 3 * KT + 1))
            inner(U_AT + 1, 1, (0, 24), q2_ready, 0)
            inner(U_AT + 2, 0, (0, 24), k2_ready, 1)


            def fill(j, *parts):
                if j + 2 < pairs:
                    inner(U_AT + 2 * j + 4, 0, parts[0], k2_ready, j + 2)
                else:
                    for uu, s, k2s in parts[j + 3 - pairs]:
                        pe.wait_ge(lo_ready, U_WO + uu + 1)
                        pe.wait_ge(ot_l, 2 * uu + max(k2s) + 1 + 1)
                        if uu == 0 and 0 in k2s:
                            pe.wait_ge((k2_ready, q2_ready)[s], pairs)
                        node_tile(uu, uu, RING, XT, 0, bank[s], s, k2s)

            both = (0, 1)
            pe.wait_ge(v2_lo, 2 * NT)
            for s in range(NT):
                scores(0, s)
            for j in range(pairs):
                a, b = 2 * j, 2 * j + 1
                if j + 1 < pairs:
                    inner(U_AT + 2 * j + 3, 1, (0, 8), q2_ready, j + 1)
                else:
                    fill(j, (), (), [(1, 0, both)])
                for s in range(NT):
                    scores(b, s)
                if j + 1 < pairs:
                    inner(U_AT + 2 * j + 3, 1, (8, 24), q2_ready, j + 1)
                fill(j, (0, 15), [(0, 0, both)], [(1, 1, both)])
                for m in range(NT):
                    turn_probs(a, m)
                fill(j, (15, 20), [(0, 1, both)], [(2, 0, both)])
                weigh(a)
                for m in range(NT):
                    turn_probs(b, m)
                fill(j, (20, 24), [], [])
                if j + 1 < pairs:
                    for s in range(NT):
                        scores(b + 1, s)
                else:
                    fill(j, (), (), [(2, 1, both)])
                weigh(b)

            for uu in range(RING):
                pe.wait_ge(lo_ready, U_WO + uu + 1)
                pe.wait_ge(ot_l, 2 * uu + 2 + 1)
                if uu == RING - 1:
                    for s in range(2):
                        node_tile(uu, uu, RING, XT, 0, bank[s], s).then_inc(tok_done, 1)
                node_tile(uu, uu, RING, XT, 0, bank[2], 2).then_inc(unit_used, 1)
            for uu in range(2):
                pe.wait_ge(lo_ready, U_WO + RING + uu + 1)
                by_nodes(uu, uu, RING, XT, 0, bank[3:6])

            def sum_counts(u):
                pe.wait_ge(checked, u - U_F1 + 1)
                nc.tensor.matmul(flag_cell(u), inexact[:, u - U_F1:u - U_F1 + 1], ones[:], start=True, stop=True,
                                 skip_group_check=True).then_inc(summed, 1)

            def where_inexact(u, products):
                pe.wait_ge(flag_ready, u - U_F1 + 1)
                count = pe.value_load(flags[0:1, u - U_F1:u - U_F1 + 1])
                with pe.If(count != 0):
                    products()

            for s in range(NT):
                if s == 1:
                    sum_counts(U_F1)
                for uu in range(2, RING):
                    pe.wait_ge(lo_ready, U_WO + RING + uu + 1)
                    last = node_tile(uu, uu, RING, XT, 0, bank[3 + s], s)
                    if s == NT - 1:
                        last.then_inc(unit_used, 1)
                if s < NT - 1:
                    last.then_inc(tok_done, 1)
            turn(1)

            def ffn_tile(u, offset, kt, acts, a0, dst, parts, ready, sums=()):
                def columns(k):
                    return slice(offset + k * P, offset + (k + 1) * P)

                def low():
                    for k in range(kt):
                        nc.tensor.matmul(dst[:, 0:NODES], w_lo[:, u % RING, columns(k)], acts[0][:, a0 + k],
                                         start=False, stop=False)

                for k in parts:
                    pe.wait_ge(ready[0], ready[1] + k)
                    for m in range(2):
                        if k == kt - 1 and m == 1:
                            if sums:
                                pe.wait_ge(flag_ready, u - U_F1 + 1)
                            for v in sums:
                                sum_counts(v)
                            where_inexact(u, low)
                        last = nc.tensor.matmul(dst[:, 0:NODES], w_hi[:, u % RING, columns(k)], acts[m][:, a0 + k],
                                                start=k == 0 and m == 0, stop=k == kt - 1 and m == 1)
                return last

            for j in range(4):
                for n in range(2):
                    u = U_F1 + 2 * j + n
                    pe.wait_ge(lo_ready, u + 1)
                    if j >= 2:
                        pe.wait_ge(f_mul, j - 1)
                    ffn_tile(u, 0, KT, XT, 0, bank[2 * (j % 2) + n], range(KT), (act_lo, 4 * KT + 1),
                             (u + 1,)).then_inc(unit_used, 1)

            def hidden(n, parts):
                u = U_H1 + (n - 4) // 2
                pe.wait_ge(lo_ready, u + 1)
                layer = 0 if n < 8 else 4
                last = ffn_tile(u, HALF * (n % 2), 4, QK, layer, bank[n % 4], parts, (f_lo, layer + 1),
                                () if n % 2 else (u + 1,))
                if 3 in parts:
                    last.then_inc(unit_used if n % 2 else h_done, 1)

            for n in (4, 8):
                hidden(n, range(3))
                hidden(n + 1, range(3))
                hidden(n, (3,))
                hidden(n + 1, (3,))
                hidden(n + 2, range(4))
                hidden(n + 3, range(4))
            for h in range(2):
                for pair in range(2):
                    u = U_W3 + 2 * h + pair
                    banks = bank[5 - 3 * h:8 - 3 * h]
                    pe.wait_ge(lo_ready, u + 1)
                    pe.wait_ge(f_lo, 10 + 2 * pair)

                    def part(s, k2, m):
                        a, w = ((0, w_hi), (1, w_hi), (0, w_lo))[m]
                        return nc.tensor.matmul(banks[s][:], QK[a][:, 8 + 2 * pair + k2, s * P:(s + 1) * P],
                                                w[:, u % RING, k2 * HALF:(k2 + 1) * HALF],
                                                start=pair == k2 == m == 0, stop=pair == k2 == m == 1)

                    def low():
                        for s in range(NT):
                            for k2 in range(2):
                                part(s, k2, 2)

                    if u < U_W3 + 2:
                        pe.wait_ge(flag_ready, u - U_F1 + 1)
                        for v in range(u + 1, 2 * u - U_W3 + 2):
                            sum_counts(v)
                    if pair == 0:
                        for s in range(NT):
                            part(s, 0, 0)
                    where_inexact(u, low)
                    for s in range(NT):
                        for k2 in range(2):
                            for m in range(2):
                                if pair or k2 or m:
                                    last = part(s, k2, m)
                        if pair == 1 and s < NT - 1:
                            last.then_inc(tok_done, 1)
                    last.then_inc(unit_used, 1)


def host_units(w):
    import numpy as np

    def by_weight(a):
        o, i = a.shape
        per = FEAT // i
        return a.reshape(o // P // per, per, P, i // P, P).transpose(0, 4, 1, 3, 2).reshape(-1, P, FEAT)

    def by_nodes(a):
        o, i = a.shape
        return a.reshape(o // HALF, HALF, i // (2 * P), 2, P).transpose(0, 2, 4, 3, 1).reshape(-1, P, FEAT)

    def in_turn(a, b):
        return np.stack([by_weight(a), by_weight(b)], axis=1).reshape(-1, P, FEAT)

    units = [by_weight(w["L0_gnn_wv"]), by_nodes(w["L0_gnn_wiv"]), by_weight(w["L0_gnn_wq"]), by_weight(w["L0_gnn_wk"]),
             in_turn(w["L0_gnn_wik"], w["L0_gnn_wiq"]), by_nodes(w["L0_gnn_wo"]), in_turn(w["L0_ffn_w1_w"], w["L0_ffn_w2_w"]),
             by_weight(w["L0_ffn_h1_w"]), by_weight(w["L0_ffn_h2_w"]), by_nodes(w["L0_ffn_w3_w"])]
    return np.ascontiguousarray(np.concatenate(units))


def host_cols(w):
    import numpy as np

    def tiles(a):
        return a.reshape(-1, P).T

    def heads(a):
        return np.concatenate([a.reshape(HEADS, HD).T] * 2)

    return np.ascontiguousarray(np.concatenate(
        [tiles(w["L0_gnn_bv"]), tiles(w["L0_gnn_bq"]), tiles(w["L0_gnn_bk"]), heads(w["L0_gnn_biq"]),
         heads(w["L0_gnn_bik"]), heads(w["L0_gnn_biv"]), tiles(w["L0_ffn_w1_s"]), tiles(w["L0_ffn_w2_s"]),
         tiles(w["L0_ffn_h1_s"]), tiles(w["L0_ffn_h2_s"])], axis=1))


def kernel(**inputs):
    import numpy as np
    import concourse.bacc as bacc
    from concourse.bass_utils import run_bass_kernel_spmd

    w = {name: np.asarray(a) for name, a in inputs.items()}
    e = [w["src"], w["dst"], w["edge_type_5"]]
    arrays = {
        "x": np.ascontiguousarray(w["x"]),
        "src_dst": np.stack(e[:2]).reshape(2, P, ETILES),
        "edge_cols": np.ascontiguousarray(np.stack(e).reshape(3, ETILES, P).transpose(2, 0, 1)),
        "etw": np.ascontiguousarray(w["L0_gnn_edge_type_weights"]),
        "weights": host_units(w),
        "cols": host_cols(w),
        "bo": np.ascontiguousarray(w["L0_gnn_bo"]),
        "w3_s": np.ascontiguousarray(w["L0_ffn_w3_s"]),
    }
    nc = bacc.Bacc("TRN2", target_bir_lowering=False, num_devices=1)
    args = [nc.dram_tensor(f"in_{n}", a.shape, mybir.dt.from_np(a.dtype), kind="ExternalInput").ap() for n, a in arrays.items()]
    codes = nc.dram_tensor("codes", (EDGES,), F32, kind="Internal").ap()
    table = nc.dram_tensor("table", (CELLS + WINDOW * P, 1), F32, kind="Internal").ap()
    out = nc.dram_tensor("out", (NODES, FEAT), F32, kind="ExternalOutput").ap()
    gnn_ffn(nc, *args, codes, table, out)
    r = run_bass_kernel_spmd(nc, [{f"in_{n}": a for n, a in arrays.items()}], core_ids=[0])
    return r.results[0]["out"]
```
